# Optimizing a Trainium2 kernel written in Bass

```python
import numpy as np
import jax
import jax.numpy as jnp

def _softmax(x, axis=-1):
    return jax.nn.softmax(x, axis=axis)

def _gelu(x):
    return jax.nn.gelu(x, approximate=True)

def _silu(x):
    return jax.nn.silu(x)

def _sigmoid(x):
    return jax.nn.sigmoid(x)

def _layernorm(x, axis=-1, eps=1e-05):
    m = jnp.mean(x, axis=axis, keepdims=True)
    v = jnp.var(x, axis=axis, keepdims=True)
    return (x - m) / jnp.sqrt(v + eps)

def _scatter_add(tgt, idx, src, axis=0):
    return tgt.at[idx].add(src)

def _segment_sum(src, seg, n):
    return jax.ops.segment_sum(src, seg, n)
kernel_name = 'mk_decoder_preln_d2_seqx_r4_871ee4'

def setup_inputs(seed: int=0):
    np.random.seed(seed)
    _w = jnp.asarray

    def _rec_inputs():
        import jax
        import jax.numpy as jnp
        _rk = jax.random.key(seed)
        x = -0.0003929 + 0.9999 * jax.random.normal(jax.random.fold_in(_rk, 1), (8, 100, 256), jnp.float32)
        _lenS = 100 - jax.random.randint(jax.random.fold_in(_rk, 7), (8,), 0, max(1, 100 // 4) + 1, jnp.int32)
        _lenS2 = 361 - jax.random.randint(jax.random.fold_in(_rk, 8), (8,), 0, max(1, 361 // 4) + 1, jnp.int32)
        _ctx_1024P = jax.random.normal(jax.random.fold_in(_rk, 11), (8, 16, 256), jnp.float32)
        _ctx_1024c = jax.random.dirichlet(jax.random.fold_in(_rk, 511), 0.3 * jnp.ones((16,), jnp.float32), (8, 361))
        _ctx_1024t = jnp.einsum('bsk,bkd->bsd', _ctx_1024c, _ctx_1024P)
        _ctx_1024t = _ctx_1024t * jax.lax.rsqrt(jnp.mean(jnp.square(_ctx_1024t)) + 1e-12) * 0.953939
        ctx_1024 = 2.81802e-05 + 1.00001 * (_ctx_1024t + 0.3 * jax.random.normal(jax.random.fold_in(_rk, 611), (8, 361, 256), jnp.float32))
        _validS = jnp.arange(100)[None, :] < _lenS[:, None]
        _validS2 = jnp.arange(361)[None, :] < _lenS2[:, None]
        _causal = jnp.tril(jnp.ones((100, 100), dtype=bool))
        mask_BxS2_ik1 = jnp.where(jnp.broadcast_to(_validS2[:, :], (8, 361)), 1, 0).astype(jnp.int32)
        mask_BxS2_bk0 = jnp.logical_not(jnp.broadcast_to(_validS2[:, :], (8, 361)))
        return (x, ctx_1024, mask_BxS2_ik1, mask_BxS2_bk0)
    x, ctx_1024, mask_BxS2_ik1, mask_BxS2_bk0 = _rec_inputs()

    def _L0_attn_setup():
        import jax, jax.numpy as jnp
        import numpy as np
        D_MODEL = 256
        NHEAD = 16
        HEAD_DIM = D_MODEL // NHEAD
        NPOS_MAX = 250
        SEQ = 256
        BATCH = 4

        def _cope(query, attn_logits, pos_emb):
            gates = jax.nn.sigmoid(attn_logits)
            pos = jnp.cumsum(gates[..., ::-1], axis=-1)[..., ::-1]
            pos = jnp.minimum(pos, NPOS_MAX - 1)
            pos_ceil = jnp.ceil(pos).astype(jnp.int32)
            pos_floor = jnp.floor(pos).astype(jnp.int32)
            logits_int = jnp.einsum('hbsd,dn->hbsn', query, pos_emb[0])
            logits_ceil = jnp.take_along_axis(logits_int, pos_ceil, axis=-1)
            logits_floor = jnp.take_along_axis(logits_int, pos_floor, axis=-1)
            w = pos - pos_floor.astype(pos.dtype)
            return logits_ceil * w + logits_floor * (1.0 - w)
        key = jax.random.key(seed)
        ks = jax.random.split(key, 10)
        s = 0.02
        return {'x': jax.random.normal(ks[0], (SEQ, BATCH, D_MODEL), dtype=jnp.float32), 'Wq': jax.random.normal(ks[1], (D_MODEL, D_MODEL), dtype=jnp.float32) * s, 'bq': jnp.zeros((D_MODEL,), dtype=jnp.float32), 'Wk': jax.random.normal(ks[2], (D_MODEL, D_MODEL), dtype=jnp.float32) * s, 'bk': jnp.zeros((D_MODEL,), dtype=jnp.float32), 'Wv': jax.random.normal(ks[3], (D_MODEL, D_MODEL), dtype=jnp.float32) * s, 'bv': jnp.zeros((D_MODEL,), dtype=jnp.float32), 'Wo': jax.random.normal(ks[4], (D_MODEL, D_MODEL), dtype=jnp.float32) * s, 'bo': jnp.zeros((D_MODEL,), dtype=jnp.float32), 'pos_emb': jax.random.normal(ks[5], (1, HEAD_DIM, NPOS_MAX), dtype=jnp.float32) * s}
    _L0_attn_all = _L0_attn_setup()
    _L0_attn_in = {k: v for k, v in _L0_attn_all.items() if k in ('Wq', 'bq', 'Wk', 'bk', 'Wv', 'bv', 'Wo', 'bo', 'pos_emb')}
    del _L0_attn_all

    def _L0_xattn_setup():
        import jax, jax.numpy as jnp
        import numpy as np
        D_MODEL = 256
        OUT = 256
        BS, SEQ = (8, 512)
        key = jax.random.key(seed)
        ks = jax.random.split(key, 11)
        scale = 1.0 / np.sqrt(D_MODEL)
        return {'q': jax.random.normal(ks[0], (BS, SEQ, D_MODEL), dtype=jnp.float32), 'k': jax.random.normal(ks[1], (BS, SEQ, D_MODEL), dtype=jnp.float32), 'v': jax.random.normal(ks[2], (BS, SEQ, D_MODEL), dtype=jnp.float32), 'Wq': jax.random.normal(ks[3], (D_MODEL, OUT), dtype=jnp.float32) * scale, 'bq': jnp.zeros((OUT,), dtype=jnp.float32), 'Wk': jax.random.normal(ks[4], (D_MODEL, OUT), dtype=jnp.float32) * scale, 'bk': jnp.zeros((OUT,), dtype=jnp.float32), 'Wv': jax.random.normal(ks[5], (D_MODEL, OUT), dtype=jnp.float32) * scale, 'bv': jnp.zeros((OUT,), dtype=jnp.float32), 'mask': jax.random.randint(ks[6], (BS, SEQ), 0, 2, dtype=jnp.int32)}
    _L0_xattn_all = _L0_xattn_setup()
    _L0_xattn_in = {k: v for k, v in _L0_xattn_all.items() if k in ('Wq', 'bq', 'Wk', 'bk', 'Wv', 'bv')}
    del _L0_xattn_all

    def _L0_ffn_setup():
        import jax, jax.numpy as jnp
        import numpy as np
        key = jax.random.key(seed)
        ks = jax.random.split(key, 5)
        B, T, D, E = (4, 512, 256, 8)
        inputs = jax.random.normal(ks[0], (B, T, D), dtype=jnp.float32)
        Wr = jax.random.normal(ks[1], (D, E), dtype=jnp.float32) * 0.02
        br = jnp.zeros((E,), dtype=jnp.float32)
        W1 = jax.random.normal(ks[2], (E, D, D), dtype=jnp.float32) * 0.02
        b1 = jnp.zeros((E, D), dtype=jnp.float32)
        W2 = jax.random.normal(ks[3], (E, D, D), dtype=jnp.float32) * 0.02
        b2 = jnp.zeros((E, D), dtype=jnp.float32)
        return {'inputs': inputs, 'Wr': Wr, 'br': br, 'W1': W1, 'b1': b1, 'W2': W2, 'b2': b2}
    _L0_ffn_all = _L0_ffn_setup()
    _L0_ffn_in = {k: v for k, v in _L0_ffn_all.items() if k in ('Wr', 'br', 'W1', 'b1', 'W2', 'b2')}
    del _L0_ffn_all

    def _L1_attn_setup():
        import jax, jax.numpy as jnp
        import numpy as np
        D_MODEL = 256
        N_HEADS = 16
        D_HEAD = 64
        D_REC = N_HEADS * D_HEAD
        BATCH = 4
        SEQ = 2048
        CHUNK = 64

        def _make_decay_bias():
            n_fast, n_medium, n_slow = (5, 6, 5)
            b = np.zeros(D_REC, dtype=np.float32)
            fast_end = n_fast * D_HEAD
            medium_end = (n_fast + n_medium) * D_HEAD
            b[:fast_end] = -2.2
            b[fast_end:medium_end] = 0.0
            b[medium_end:] = 4.6
            return jnp.asarray(b)

        def _chunked_scan(decay, value, chunk_size=CHUNK):
            b, s, d = decay.shape
            pad = -s % chunk_size
            if pad:
                decay = jnp.pad(decay, ((0, 0), (0, pad), (0, 0)), constant_values=1.0)
                value = jnp.pad(value, ((0, 0), (0, pad), (0, 0)))
            total = s + pad
            n = total // chunk_size
            dc = decay.reshape(b, n, chunk_size, d)
            vc = value.reshape(b, n, chunk_size, d)
            cum_log = jnp.cumsum(jnp.log(jnp.maximum(dc, 1e-10)), axis=2)
            cum_decay = jnp.exp(cum_log)
            weighted = vc / jnp.maximum(cum_decay, 1e-10)
            intra_state = cum_decay * jnp.cumsum(weighted, axis=2)
            chunk_final_state = intra_state[:, :, -1, :]
            chunk_total_decay = cum_decay[:, :, -1, :]
            cum_log_chunk = jnp.cumsum(jnp.log(jnp.maximum(chunk_total_decay, 1e-10)), axis=1)
            cum_chunk_decay = jnp.exp(cum_log_chunk)
            cum_weighted_chunk = jnp.cumsum(chunk_final_state / jnp.maximum(cum_chunk_decay, 1e-10), axis=1)
            zeros = jnp.zeros((b, 1, d), dtype=cum_weighted_chunk.dtype)
            ones = jnp.ones((b, 1, d), dtype=cum_chunk_decay.dtype)
            incoming_cum_weighted = jnp.concatenate([zeros, cum_weighted_chunk[:, :-1]], axis=1)
            incoming_cum_decay = jnp.concatenate([ones, cum_chunk_decay[:, :-1]], axis=1)
            incoming_state = incoming_cum_decay * incoming_cum_weighted
            cross_contrib = cum_decay * incoming_state[:, :, None, :]
            states = (intra_state + cross_contrib).reshape(b, total, d)[:, :s]
            return states
        key = jax.random.key(seed)
        k_x, k_w1, k_w2 = jax.random.split(key, 3)
        x = jax.random.normal(k_x, (BATCH, SEQ, D_MODEL), dtype=jnp.float32)
        W_aiv = jax.random.normal(k_w1, (D_MODEL, 3 * D_REC), dtype=jnp.float32) / np.sqrt(D_MODEL)
        decay_bias = _make_decay_bias()
        W_mix = jax.random.normal(k_w2, (D_REC, D_MODEL), dtype=jnp.float32) / np.sqrt(D_REC)
        b_mix = jnp.zeros((D_MODEL,), dtype=jnp.float32)
        return {'x': x, 'W_aiv': W_aiv, 'decay_bias': decay_bias, 'W_mix': W_mix, 'b_mix': b_mix}
    _L1_attn_all = _L1_attn_setup()
    _L1_attn_in = {k: v for k, v in _L1_attn_all.items() if k in ('W_aiv', 'decay_bias', 'W_mix', 'b_mix')}
    del _L1_attn_all

    def _L1_xattn_setup():
        import jax, jax.numpy as jnp
        import numpy as np
        B, T, D, H = (2, 512, 256, 16)
        DK = D // H

        def _split_heads(x):
            b, s, _ = x.shape
            return x.reshape(b, s, H, DK).transpose(0, 2, 1, 3)
        key = jax.random.key(seed)
        ks = jax.random.split(key, 12)
        s = 0.02
        return {'query': jax.random.normal(ks[0], (B, T, D), jnp.float32), 'key': jax.random.normal(ks[1], (B, T, D), jnp.float32), 'value': jax.random.normal(ks[2], (B, T, D), jnp.float32), 'mask': jax.random.randint(ks[3], (B, T), 0, 2) != 0, 'Wq': jax.random.normal(ks[4], (D, D), jnp.float32) * s, 'bq': jnp.zeros((D,), jnp.float32), 'Wk': jax.random.normal(ks[5], (D, D), jnp.float32) * s, 'bk': jnp.zeros((D,), jnp.float32), 'Wv': jax.random.normal(ks[6], (D, D), jnp.float32) * s, 'bv': jnp.zeros((D,), jnp.float32), 'Wo': jax.random.normal(ks[7], (D, D), jnp.float32) * s, 'bo': jnp.zeros((D,), jnp.float32)}
    _L1_xattn_all = _L1_xattn_setup()
    _L1_xattn_in = {k: v for k, v in _L1_xattn_all.items() if k in ('Wq', 'bq', 'Wk', 'bk', 'Wv', 'bv', 'Wo', 'bo')}
    del _L1_xattn_all

    def _L1_ffn_setup():
        import jax, jax.numpy as jnp
        import numpy as np
        EPS = 1e-05

        @jax.custom_vjp
        def ste_quantize(w):
            scale = jnp.maximum(jnp.mean(jnp.abs(w)), EPS)
            return jnp.clip(jnp.round(w / scale), -1.0, 1.0)

        def _ste_fwd(w):
            return (ste_quantize(w), None)

        def _ste_bwd(_, g):
            return (g,)
        ste_quantize.defvjp(_ste_fwd, _ste_bwd)
        key = jax.random.key(seed)
        k1, k2 = jax.random.split(key)
        x = jax.random.normal(k1, (8, 2048, 256), dtype=jnp.float32)
        weight = jax.random.normal(k2, (256, 256), dtype=jnp.float32) * 0.02
        return {'x': x, 'weight': weight}
    _L1_ffn_all = _L1_ffn_setup()
    _L1_ffn_in = {k: v for k, v in _L1_ffn_all.items() if k in ('weight',)}
    del _L1_ffn_all
    return {'x': x, 'ctx_1024': ctx_1024, 'mask_BxS2_ik1': mask_BxS2_ik1, 'mask_BxS2_bk0': mask_BxS2_bk0, 'L0_attn_Wq': _L0_attn_in['Wq'], 'L0_attn_bq': _L0_attn_in['bq'], 'L0_attn_Wk': _L0_attn_in['Wk'], 'L0_attn_bk': _L0_attn_in['bk'], 'L0_attn_Wv': _L0_attn_in['Wv'], 'L0_attn_bv': _L0_attn_in['bv'], 'L0_attn_Wo': _L0_attn_in['Wo'], 'L0_attn_bo': _L0_attn_in['bo'], 'L0_attn_pos_emb': _L0_attn_in['pos_emb'], 'L0_xattn_Wq': _L0_xattn_in['Wq'], 'L0_xattn_bq': _L0_xattn_in['bq'], 'L0_xattn_Wk': _L0_xattn_in['Wk'], 'L0_xattn_bk': _L0_xattn_in['bk'], 'L0_xattn_Wv': _L0_xattn_in['Wv'], 'L0_xattn_bv': _L0_xattn_in['bv'], 'L0_ffn_Wr': _L0_ffn_in['Wr'], 'L0_ffn_br': _L0_ffn_in['br'], 'L0_ffn_W1': _L0_ffn_in['W1'], 'L0_ffn_b1': _L0_ffn_in['b1'], 'L0_ffn_W2': _L0_ffn_in['W2'], 'L0_ffn_b2': _L0_ffn_in['b2'], 'L1_attn_W_aiv': _L1_attn_in['W_aiv'], 'L1_attn_decay_bias': _L1_attn_in['decay_bias'], 'L1_attn_W_mix': _L1_attn_in['W_mix'], 'L1_attn_b_mix': _L1_attn_in['b_mix'], 'L1_xattn_Wq': _L1_xattn_in['Wq'], 'L1_xattn_bq': _L1_xattn_in['bq'], 'L1_xattn_Wk': _L1_xattn_in['Wk'], 'L1_xattn_bk': _L1_xattn_in['bk'], 'L1_xattn_Wv': _L1_xattn_in['Wv'], 'L1_xattn_bv': _L1_xattn_in['bv'], 'L1_xattn_Wo': _L1_xattn_in['Wo'], 'L1_xattn_bo': _L1_xattn_in['bo'], 'L1_ffn_weight': _L1_ffn_in['weight']}

def reference(x, ctx_1024, mask_BxS2_ik1, mask_BxS2_bk0, L0_attn_Wq, L0_attn_bq, L0_attn_Wk, L0_attn_bk, L0_attn_Wv, L0_attn_bv, L0_attn_Wo, L0_attn_bo, L0_attn_pos_emb, L0_xattn_Wq, L0_xattn_bq, L0_xattn_Wk, L0_xattn_bk, L0_xattn_Wv, L0_xattn_bv, L0_ffn_Wr, L0_ffn_br, L0_ffn_W1, L0_ffn_b1, L0_ffn_W2, L0_ffn_b2, L1_attn_W_aiv, L1_attn_decay_bias, L1_attn_W_mix, L1_attn_b_mix, L1_xattn_Wq, L1_xattn_bq, L1_xattn_Wk, L1_xattn_bk, L1_xattn_Wv, L1_xattn_bv, L1_xattn_Wo, L1_xattn_bo, L1_ffn_weight):
    import jax
    import jax.numpy as jnp

    def _L0_attn_ref(x, Wq, bq, Wk, bk, Wv, bv, Wo, bo, pos_emb):
        import jax, jax.numpy as jnp
        import numpy as np
        D_MODEL = 256
        NHEAD = 16
        HEAD_DIM = D_MODEL // NHEAD
        NPOS_MAX = 250
        SEQ = 256
        BATCH = 4

        def _cope(query, attn_logits, pos_emb):
            gates = jax.nn.sigmoid(attn_logits)
            pos = jnp.cumsum(gates[..., ::-1], axis=-1)[..., ::-1]
            pos = jnp.minimum(pos, NPOS_MAX - 1)
            pos_ceil = jnp.ceil(pos).astype(jnp.int32)
            pos_floor = jnp.floor(pos).astype(jnp.int32)
            logits_int = jnp.einsum('hbsd,dn->hbsn', query, pos_emb[0])
            logits_ceil = jnp.take_along_axis(logits_int, pos_ceil, axis=-1)
            logits_floor = jnp.take_along_axis(logits_int, pos_floor, axis=-1)
            w = pos - pos_floor.astype(pos.dtype)
            return logits_ceil * w + logits_floor * (1.0 - w)
        S, B, _ = x.shape

        def split_heads(t):
            return t.reshape(S, B, NHEAD, HEAD_DIM).transpose(2, 1, 0, 3)
        q = split_heads(x @ Wq + bq)
        k = split_heads(x @ Wk + bk)
        v = split_heads(x @ Wv + bv)
        scale = 1.0 / HEAD_DIM ** 0.5
        attn_logits = jnp.einsum('hbsd,hbtd->hbst', q, k) * scale
        attn_logits = attn_logits + _cope(q, attn_logits, pos_emb)
        attn = jax.nn.softmax(attn_logits, axis=-1)
        out = jnp.einsum('hbst,hbtd->hbsd', attn, v)
        out = out.transpose(2, 1, 0, 3).reshape(S, B, D_MODEL)
        return out @ Wo + bo

    def _L0_xattn_ref(q, k, v, Wq, bq, Wk, bk, Wv, bv, mask):
        import jax, jax.numpy as jnp
        import numpy as np
        D_MODEL = 256
        OUT = 256
        BS, SEQ = (8, 512)
        query = q @ Wq + bq
        key_p = k @ Wk + bk
        value = v @ Wv + bv
        dim_k = key_p.shape[-1]
        scores = jnp.einsum('btd,bsd->bts', query, key_p) / jnp.sqrt(jnp.asarray(dim_k, dtype=query.dtype))
        scores = jnp.where(mask[:, None, :] == 0, -jnp.inf, scores)
        weights = jax.nn.softmax(scores, axis=-1)
        outputs = jnp.einsum('bts,bsd->btd', weights, value)
        return outputs

    def _L0_ffn_ref(inputs, Wr, br, W1, b1, W2, b2):
        import jax, jax.numpy as jnp
        import numpy as np
        B, T, D = inputs.shape
        E = Wr.shape[1]
        x = inputs.reshape(B * T, D)
        N = x.shape[0]
        C = N // E
        logits = x @ Wr + br
        probs = jax.nn.softmax(logits, axis=-1)
        gate = jnp.max(probs, axis=-1, keepdims=True)
        idx = jnp.argmax(probs, axis=-1)
        mask = jax.nn.one_hot(idx, E, dtype=jnp.float32)
        pos = (jnp.cumsum(mask, axis=0) * mask).astype(jnp.int32)
        mask = mask * (pos < C).astype(jnp.float32)
        mask_flat = jnp.sum(mask, axis=-1, keepdims=True)
        gate = gate * mask_flat
        combine = (gate * mask_flat * jax.nn.one_hot(idx, E, dtype=jnp.float32))[..., None] * jax.nn.one_hot(pos, C, dtype=jnp.float32)
        dispatch = combine
        expert_in = jnp.einsum('nd,nec->ecd', x, dispatch)
        h = jax.nn.relu(jnp.einsum('ecd,edf->ecf', expert_in, W1) + b1[:, None, :])
        eo = jnp.einsum('ecf,efd->ecd', h, W2) + b2[:, None, :]
        out = jnp.einsum('ecd,nec->nd', eo, combine)
        return out.reshape(B, T, D)

    def _L1_attn_ref(x, W_aiv, decay_bias, W_mix, b_mix):
        import jax, jax.numpy as jnp
        import numpy as np
        D_MODEL = 256
        N_HEADS = 16
        D_HEAD = 64
        D_REC = N_HEADS * D_HEAD
        BATCH = 4
        SEQ = 2048
        CHUNK = 64

        def _make_decay_bias():
            n_fast, n_medium, n_slow = (5, 6, 5)
            b = np.zeros(D_REC, dtype=np.float32)
            fast_end = n_fast * D_HEAD
            medium_end = (n_fast + n_medium) * D_HEAD
            b[:fast_end] = -2.2
            b[fast_end:medium_end] = 0.0
            b[medium_end:] = 4.6
            return jnp.asarray(b)

        def _chunked_scan(decay, value, chunk_size=CHUNK):
            b, s, d = decay.shape
            pad = -s % chunk_size
            if pad:
                decay = jnp.pad(decay, ((0, 0), (0, pad), (0, 0)), constant_values=1.0)
                value = jnp.pad(value, ((0, 0), (0, pad), (0, 0)))
            total = s + pad
            n = total // chunk_size
            dc = decay.reshape(b, n, chunk_size, d)
            vc = value.reshape(b, n, chunk_size, d)
            cum_log = jnp.cumsum(jnp.log(jnp.maximum(dc, 1e-10)), axis=2)
            cum_decay = jnp.exp(cum_log)
            weighted = vc / jnp.maximum(cum_decay, 1e-10)
            intra_state = cum_decay * jnp.cumsum(weighted, axis=2)
            chunk_final_state = intra_state[:, :, -1, :]
            chunk_total_decay = cum_decay[:, :, -1, :]
            cum_log_chunk = jnp.cumsum(jnp.log(jnp.maximum(chunk_total_decay, 1e-10)), axis=1)
            cum_chunk_decay = jnp.exp(cum_log_chunk)
            cum_weighted_chunk = jnp.cumsum(chunk_final_state / jnp.maximum(cum_chunk_decay, 1e-10), axis=1)
            zeros = jnp.zeros((b, 1, d), dtype=cum_weighted_chunk.dtype)
            ones = jnp.ones((b, 1, d), dtype=cum_chunk_decay.dtype)
            incoming_cum_weighted = jnp.concatenate([zeros, cum_weighted_chunk[:, :-1]], axis=1)
            incoming_cum_decay = jnp.concatenate([ones, cum_chunk_decay[:, :-1]], axis=1)
            incoming_state = incoming_cum_decay * incoming_cum_weighted
            cross_contrib = cum_decay * incoming_state[:, :, None, :]
            states = (intra_state + cross_contrib).reshape(b, total, d)[:, :s]
            return states
        aiv = x @ W_aiv
        a_proj, i_proj, v = jnp.split(aiv, 3, axis=-1)
        a = jax.nn.sigmoid(a_proj + decay_bias)
        i = jax.nn.sigmoid(i_proj)
        input_signal = jnp.sqrt(jnp.maximum(1.0 - a * a, 1e-08)) * (i * v)
        h = _chunked_scan(a.astype(jnp.float32), input_signal.astype(jnp.float32))
        h = h.astype(x.dtype)
        return h @ W_mix + b_mix

    def _L1_xattn_ref(query, key, value, mask, Wq, bq, Wk, bk, Wv, bv, Wo, bo):
        import jax, jax.numpy as jnp
        import numpy as np
        B, T, D, H = (2, 512, 256, 16)
        DK = D // H

        def _split_heads(x):
            b, s, _ = x.shape
            return x.reshape(b, s, H, DK).transpose(0, 2, 1, 3)
        q = _split_heads(query @ Wq.T + bq)
        k = _split_heads(key @ Wk.T + bk)
        v = _split_heads(value @ Wv.T + bv)
        scale = 1.0 / np.sqrt(DK).astype(np.float32)
        scores = jnp.einsum('bhtd,bhsd->bhts', q, k) * scale
        scores = jnp.where(mask[:, None, None, :], scores, -jnp.inf)
        attn = jax.nn.softmax(scores, axis=-1)
        out = jnp.einsum('bhts,bhsd->bhtd', attn, v)
        out = out.transpose(0, 2, 1, 3).reshape(query.shape[0], -1, D)
        return out @ Wo.T + bo

    def _L1_ffn_ref(x, weight):
        import jax, jax.numpy as jnp
        import numpy as np
        EPS = 1e-05

        @jax.custom_vjp
        def ste_quantize(w):
            scale = jnp.maximum(jnp.mean(jnp.abs(w)), EPS)
            return jnp.clip(jnp.round(w / scale), -1.0, 1.0)

        def _ste_fwd(w):
            return (ste_quantize(w), None)

        def _ste_bwd(_, g):
            return (g,)
        ste_quantize.defvjp(_ste_fwd, _ste_bwd)
        w_ternary = ste_quantize(weight)
        scale = jnp.maximum(jnp.mean(jnp.abs(weight)), EPS)
        return jnp.einsum('bsi,oi->bso', x, w_ternary * scale)
    x = x + _L0_attn_ref(_layernorm(x, axis=-1), L0_attn_Wq, L0_attn_bq, L0_attn_Wk, L0_attn_bk, L0_attn_Wv, L0_attn_bv, L0_attn_Wo, L0_attn_bo, L0_attn_pos_emb)
    x = x + _L0_xattn_ref(_layernorm(x, axis=-1), ctx_1024, ctx_1024, L0_xattn_Wq, L0_xattn_bq, L0_xattn_Wk, L0_xattn_bk, L0_xattn_Wv, L0_xattn_bv, mask_BxS2_ik1)
    x = x + _L0_ffn_ref(_layernorm(x, axis=-1), L0_ffn_Wr, L0_ffn_br, L0_ffn_W1, L0_ffn_b1, L0_ffn_W2, L0_ffn_b2)
    x = x + _L1_attn_ref(_layernorm(x, axis=-1), L1_attn_W_aiv, L1_attn_decay_bias, L1_attn_W_mix, L1_attn_b_mix)
    x = x + _L1_xattn_ref(_layernorm(x, axis=-1), ctx_1024, ctx_1024, mask_BxS2_bk0, L1_xattn_Wq, L1_xattn_bq, L1_xattn_Wk, L1_xattn_bk, L1_xattn_Wv, L1_xattn_bv, L1_xattn_Wo, L1_xattn_bo)
    x = x + _L1_ffn_ref(_layernorm(x, axis=-1), L1_ffn_weight)
    return x

_drawn_inputs = setup_inputs


def setup_inputs(seed=0):
    import zlib

    import numpy as np

    out = dict(_drawn_inputs(seed))
    spreads = {'L0_attn_bq': (0.0, 0.8),
     'L0_attn_bk': (0.0, 0.8),
     'L0_attn_bv': (0.0, 0.1),
     'L0_attn_bo': (0.0, 0.1),
     'L0_xattn_bq': (0.0, 0.1),
     'L0_xattn_bk': (0.0, 2.0),
     'L0_xattn_bv': (0.0, 0.1),
     'L0_ffn_br': (0.0, 0.594),
     'L0_ffn_b1': (0.0, 0.8),
     'L0_ffn_b2': (0.0, 0.555),
     'L1_attn_b_mix': (0.0, 0.1),
     'L1_xattn_bq': (0.0, 2.0),
     'L1_xattn_bk': (0.0, 2.0),
     'L1_xattn_bv': (0.0, 0.367),
     'L1_xattn_bo': (0.0, 0.1)}
    factors = {'L0_attn_Wq': 8.0,
     'L0_attn_Wk': 8.0,
     'L0_attn_pos_emb': 8.0,
     'L0_ffn_Wr': 4.497,
     'L0_ffn_W1': 8.0,
     'L0_ffn_W2': 8.0,
     'L1_xattn_Wq': 8.0,
     'L1_xattn_Wk': 8.0}
    for name, (base, spread) in spreads.items():
        noise = np.random.default_rng([zlib.crc32(name.encode()), seed]).standard_normal(out[name].shape)
        drawn = base * np.exp(spread * noise) if base else spread * noise
        out[name] = jnp.asarray(drawn.astype(out[name].dtype))
    for name, factor in factors.items():
        out[name] = (out[name] * factor).astype(out[name].dtype)
    return out
```

```python
from contextlib import ExitStack

import numpy as np

import concourse.bass as bass
from concourse import mybir

F32 = mybir.dt.float32
BF16 = mybir.dt.bfloat16
I32 = mybir.dt.int32
U32 = mybir.dt.uint32
U8 = mybir.dt.uint8
ALU = mybir.AluOpType
ACT = mybir.ActivationFunctionType
AX = mybir.AxisListType

B, T, D = 8, 100, 256
S = 361
H, DK = 16, 16
E = 8
N = B * T
CAP = N // E
P = 128
KT = D // P
HH = P // DK
G = 2
GB = B // G
GC = GB * T
EPS = 1e-5
MASKED = -1e30
REC = 1024
RT = REC // P
CHUNK = 64
TP = T + 1
FLOOR = 1e-10
NPOS = B + 1
SJ = [(0, 121), (121, 121), (242, 119)]
NJ = len(SJ)
PARTS = [(0, 0), (0, 1), (0, 2), (1, 0), (1, 1), (2, 0)]
ROW_MASK = len(PARTS) * DK
ROW_MAX = ROW_MASK + 1
KROWS = ROW_MAX + 3
HG = 4
VW = DK + 1
KSLOTS = 4
PSLOTS = 4
C_BQ0, C_BK0, C_BV0, C_BQX, C_BK1, C_BQ1, C_BV1, C_DEC, C_B1 = 0, 2, 4, 6, 8, 10, 12, 14, 22
NCB = C_B1 + 2 * E
R_BO0, R_BVX, R_BMIX, R_BO1 = range(4)
ROWBIAS = {0: R_BO0, 1: R_BVX, 3: R_BMIX, 4: R_BO1}
NBLOCKS = 6


def build(nc, a, out):
    ctx = ExitStack()
    with ctx:
        def sb(name, shape, dt=F32):
            return ctx.enter_context(nc.sbuf_tensor(name, shape, dt))

        def sem(name):
            return ctx.enter_context(nc.semaphore(name))

        def dram(name, shape, dt=F32):
            return nc.dram_tensor(name, shape, dt, kind="Internal").ap()

        PP = [ctx.enter_context(nc.psum_tensor(f"banks{i}", [P, 2, 512], F32)) for i in range(4)]
        PS = [PP[i // 2][:, i % 2] for i in range(8)]

        X = sb("X", [T, B, D])
        XN = sb("XN", [T, B, D])
        XT = sb("XT", [P, KT, N])
        identf = sb("identf", [P, P])
        identb = sb("identb", [P, P], BF16)
        onesf = sb("onesf", [P, P])
        onesb = sb("onesb", [P, P], BF16)
        tri = sb("tri", [T, T], BF16)
        selb = sb("selb", [B, B, T], BF16)
        negn = sb("negn", [P, B])
        PICK = sb("PICK", [P, HG * VW])
        ev8 = sb("ev8", [T, B, E])
        mhalf = sb("mhalf", [T, GB])
        ve = sb("ve", [T, B])
        zrow = sb("zrow", [T, D])
        CB = sb("CB", [P, NCB])
        RB = sb("RB", [T, 4, D])
        BR = sb("BR", [T, E])
        BQ16 = sb("BQ16", [P, KT])
        BQ4 = sb("BQ4", [P, KT])
        PE9 = sb("PE9", [P, NPOS])
        DD = sb("DD", [P, B])
        CF = sb("CF", [P, NPOS])
        MW = 24 + HH + 24
        M = sb("M", [P, MW])
        PEM = sb("PEM", [P, NPOS, MW])
        SELT = sb("SELT", [P, B * KT, P])
        W0 = sb("W0", [P, 4, KT, D])
        WMIX = W0[:].rearrange("p a k d -> p (a k) d")
        WX = sb("WX", [P, 3, KT, D])
        WQK = sb("WQK", [P, KT, D])
        W4 = sb("W4", [P, 4, KT, D])
        WR = sb("WR", [P, KT, E])
        WF = sb("WF", [P, KT, D])
        WN = sb("WN", [P, KT, D])
        fs = sb("fs", [P, 4])
        st6 = sb("st6", [T, B, 6])
        mv = sb("mv", [T, B, 2])
        rstd = sb("rstd", [T, B])
        mki = sb("mki", [B, S], I32)
        mkx = sb("mkx", [B, S], BF16)
        mk8 = sb("mk8", [B, S], U8)
        mk4 = sb("mk4", [B, S], BF16)
        CT = sb("CT", [P, KT, B * S])
        small = sb("small", [T, 14 * B * E])

        RA = sb("RA", [P, 8200])
        RBG = sb("RBG", [P, 2 * 3 * REC])
        RC = sb("RC", [P, 6500])
        RV = sb("RV", [P, B * NJ * H * VW])

        def part(region, at, *dims, dt=F32):
            n = int(np.prod(dims))
            words = n if dt != BF16 else (n + 1) // 2
            v = region[:, at:at + words]
            if dt != F32:
                v = v.bitcast(dt)
            names = "abcd"[:len(dims)]
            if len(dims) > 1:
                v = v.rearrange("p (" + " ".join(names) + ") -> p " + " ".join(names),
                                **dict(zip(names, dims)))
            return v

        R0 = part(RA, 0, 28 * T)
        O0 = part(RA, 2800, KT, N)
        K32 = part(RA, 4400, KT, S)
        KP = [part(RA, 5124 + 1083 * i, 3, KT, S, dt=BF16) for i in range(2)]
        PB = [part(RC, 800 * i, B, T) for i in range(5)]
        GA = part(RC, 4000, B, T)
        AC = part(RC, 4800, B, T)
        AL = part(RC, 5600, B, T)
        MX = part(RC, 6400, T)
        RS = part(RA, 7290, T)
        QKV = [part(RV, 1600 * i, KT, N) for i in range(3)]
        CN = part(RBG, 0, NJ, B, D)
        QK = part(RC, 0, KT, N)
        PX = [part(RC, 1600 + 364 * i, S) for i in range(2)]
        PT1 = [part(RC, 2400 + 300 * i, NJ, T) for i in range(2)]
        PC = part(RC, 3000, KT, N)
        W1 = part(RA, 0, E, KT, D)
        W2 = part(RA, 4096, E, KT, D)
        HT = [part(RC, 200 * i, KT, CAP) for i in range(2)]
        EO = part(RC, 400, E, D)
        B2 = part(RC, 2448, E, D)
        WA = part(RBG, 0, KT, 3 * REC)
        DEC = part(RA, 0, RT, B, TP)
        UU = part(RC, 0, RT, B, TP)
        CTF = CT[:].rearrange("p k s -> p (k s)")
        SQ = [part(CTF, 808 * i, B, TP) for i in range(4)]
        CD = part(CTF, 808 * 4, B, TP)
        BT = [part(CTF, 808 * (5 + i), B, TP) for i in range(2)]
        V4 = part(RV, 0, B * NJ, H, VW)
        KS = [part(r, H * S // 2 * i, H, S, dt=BF16) for r in (RA, RBG) for i in range(2)]
        QS = part(RC, 0, H, N, dt=BF16)
        P4 = [part(CTF, 1600 * i, H * T) for i in range(3)] + [
            part(SELT[:].rearrange("p a b -> p (a b)"), 0, H * T)]
        QW = part(CTF, 4800, KT, GC)
        QP = part(WX[:].rearrange("p a k d -> p (a k d)"), 0, 3, KT, GC, dt=BF16)
        NM = sb("NM", [T, 2, H])
        NP = sb("NP", [T, 2, 3, H], BF16)
        NT = [sb(f"NT{i}", [3 * H, T], BF16) for i in range(2)]
        ONT = PS[7][:, 0:KT * T].rearrange("p (k t) -> p k t", k=KT)
        Y4 = PS[7][:, KT * T:KT * T + D]
        NPT = PS[7][0:3 * H, 460:460 + T // 2].bitcast(BF16)
        OS = part(WQK[:].rearrange("p k d -> p (k d)"), 0, HG * T)
        RC4 = sb("RC4", [T, H])
        ON = zrow[:].rearrange("p (h d) -> p h d", h=H)
        OT = [part(PEM[:].rearrange("p n x -> p (n x)"), KT * T * i, KT, T) for i in range(2)]

        def tiny(i, n=B * E):
            return small[:, i * B * E:i * B * E + n]

        def tbe(i):
            return tiny(i).rearrange("p (b e) -> p b e", b=B)

        def tb(i):
            return tiny(i, B)

        slots_in = dram("slots_in", [N, D])
        slots_out = dram("slots_out", [N, D])
        k_parts = dram("k_parts", [3, D, B, S], BF16)
        q_parts = dram("q_parts", [3, D, N], BF16)
        mask_d = dram("mask_d", [B, S], BF16)
        ones_d = dram("ones_d", [P, P], BF16)
        zeros_d = dram("zeros_d", [T, D // 4])

        ld_x = [sem(f"ld_x{g}") for g in range(G)]
        ld = {n: sem("ld_" + n) for n in ("cb", "w0", "pe", "ct", "cn", "wx", "w4", "rows", "masks",
                                          "wr", "wf", "w1", "w2", "b2", "wa", "wmix")}
        zero_st = sem("zero_st")
        ones_st = sem("ones_st")
        mask_st = sem("mask_st")
        k_st = [sem(f"k_st{i}") for i in range(2)]
        scat = sem("scat")
        xs_ld = sem("xs_ld")
        eo_st = sem("eo_st")
        gat = [sem(f"gat{b}") for b in range(B)]
        q_st = [sem(f"q_st{g}") for g in range(G)]
        qs_ld = [sem(f"qs_ld{g}") for g in range(G)]
        qs_one = sem("qs_one")
        ks_zero = sem("ks_zero")
        ks_ld = [sem(f"ks_ld{i}") for i in range(KSLOTS)]
        nm_ld = [[sem(f"nm_{q}{i}") for i in range(2)] for q in ("sp", "pool")]
        out_st = sem("out_st")
        consts = sem("consts")
        dve_link = sem("dve_link")
        act_link = sem("act_link")
        pool_link = sem("pool_link")
        stats_done = sem("stats_done")
        aggregated = sem("aggregated")
        var_ready = sem("var_ready")
        rstd_ready = sem("rstd_ready")
        xn_ready = sem("xn_ready")
        xn_tr = sem("xn_tr")
        xt_ready = sem("xt_ready")
        bias_added = sem("bias_added")
        y_mm = sem("y_mm")
        x_new = sem("x_new")
        side_mm = sem("side_mm")
        side_out = sem("side_out")
        qkv_mm = sem("qkv_mm")
        qkv_out = sem("qkv_out")
        cope_mm = sem("cope_mm")
        prod_dve = sem("prod_dve")
        prod_pool = sem("prod_pool")
        prod_used = sem("prod_used")
        gates = sem("gates")
        pos_ready = sem("pos_ready")
        relus = sem("relus")
        shifted = sem("shifted")
        exp0 = sem("exp0")
        probs0 = sem("probs0")
        spread_mm = sem("spread_mm")
        spread_used = sem("spread_used")
        sum_dve = sem("sum_dve")
        sum_pool = sem("sum_pool")
        k_split = sem("k_split")
        v_ones = sem("v_ones")
        masks_ready = sem("masks_ready")
        wf_ready = sem("wf_ready")
        asum = sem("asum")
        qk_mm = sem("qk_mm")
        qk_out = sem("qk_out")
        sc_mm = sem("sc_mm")
        sc_max = sem("sc_max")
        sc_exp = sem("sc_exp")
        pt_mm = sem("pt_mm")
        pt_out = sem("pt_out")
        pc_mm = sem("pc_mm")
        pc_out = sem("pc_out")
        rt_mm = sem("rt_mm")
        rt_shift = sem("rt_shift")
        rt_exp = sem("rt_exp")
        onehot = sem("onehot")
        pos_mm = sem("pos_mm")
        xg_ready = sem("xg_ready")
        slots_ready = sem("slots_ready")
        xs_tr = sem("xs_tr")
        xst_ready = sem("xst_ready")
        h_mm = sem("h_mm")
        h_out = sem("h_out")
        eo_mm = sem("eo_mm")
        eo_out = sem("eo_out")
        aiv_mm = sem("aiv_mm")
        sig = sem("sig")
        clamped = sem("clamped")
        iv_done = sem("iv_done")
        squares = sem("squares")
        roots = sem("roots")
        u_done = sem("u_done")
        state = sem("state")
        pads = sem("pads")
        reset64 = sem("reset64")
        cdec = sem("cdec")
        q4_mm = sem("q4_mm")
        q4_out = sem("q4_out")
        q4_split = sem("q4_split")
        mx_mm = sem("mx_mm")
        mx_out = sem("mx_out")
        np_ready = sem("np_ready")
        np_tr = sem("np_tr")
        np_out = sem("np_out")
        st_mm = sem("st_mm")
        st_exp = sem("st_exp")
        pv_mm = sem("pv_mm")
        pv_zero = sem("pv_zero")
        os_out = sem("os_out")
        os_tr = sem("os_tr")
        on_ready = sem("on_ready")
        on_tr = sem("on_tr")
        ot_out = sem("ot_out")

        class Link:

            def __init__(self, eng, semaphore):
                self.eng, self.sem, self.n = eng, semaphore, 0

            def __call__(self, ins):
                self.n += 1
                ins.then_inc(self.sem, 1)
                self.eng.wait_ge(self.sem, self.n)

        SIDE = ([("qk", 0)] + [("k", b) for b in range(5)] + [("f", 0), ("v", 0)]
                + [x for i in range(3) for x in (("k", 5 + i), ("v", 1 + i))]
                + [("v", b) for b in range(4, B)])
        SIDE_AT = {"qkv": 1, "prod4": 2, "prod8": 3, "prod12": 4, "prod16": 5, "ln1": 8,
                   "b1_1": 9, "b1_2": 10, "b1_3": 11, "b1_4": 12, "b1_6": 13, "b1_7": 14,
                   "ln2": 15, "route": 18}

        def side_items(point, done):
            n = SIDE_AT.get(point, 0)
            items = list(range(done[0], n))
            done[0] = max(done[0], n)
            return items

        UNITS = [(s, k) for odd in range(2) for k in range(KT) for s in range(odd, B, 2)]
        POOL_UNITS = [u for u in range(len(UNITS)) if u % 4 == 3]
        DVE_UNITS = [u for u in range(len(UNITS)) if u % 4 != 3]
        PSLOT = {u: i % 3 for i, u in enumerate(DVE_UNITS)} | {u: 3 + i % 2 for i, u in enumerate(POOL_UNITS)}
        SUM_POOL = [u for u in range(2 * B) if u % 3 == 1]
        SUM_DVE = [u for u in range(2 * B) if u % 3 != 1]
        SSLOT = {u: i % 3 for i, u in enumerate(SUM_DVE)} | {u: 3 + i % 2 for i, u in enumerate(SUM_POOL)}

        PAIRS = H // 2
        UNITS4 = HG * NJ
        TICKS = 2 * PAIRS
        PLAN = ([("maxima", 2 * i, i) for i in range(PAIRS)]
                + [("parts", 21, 0)]
                + [("scores", 28 + TICKS * u // UNITS4, u) for u in range(UNITS4)]
                + [("weighted", max(35 + u // 2, 32 + TICKS * u // UNITS4), u) for u in range(UNITS4)]
                + [("os_evac", 46, 0), ("sums_tr", 49, 0), ("normalise", 49, 0), ("out_tr", 56, 0),
                   ("out_mm", 58, 0), ("add", 59, 0)])
        PLAN_END = TICKS * (B - 1) + 60
        ORDER = ("parts", "sums_tr", "normalise", "out_tr", "out_mm", "maxima", "scores", "weighted",
                 "os_evac", "add")

        def run_block4(**own):
            for tick in range(PLAN_END):
                for name in ORDER:
                    for n, at, x in PLAN:
                        b = (tick - at) // TICKS
                        if n == name and name in own and (tick - at) % TICKS == 0 and 0 <= b < B:
                            own[name](b, x)

        def load_maxima(queue, b, i):
            queue.dma_start(QS[ROW_MAX + i:ROW_MAX + i + 1, :, b * T:b * T + T],
                            NT[b % 2][H * i:H * i + H]).then_inc(nm_ld[i == 2][b % 2], 16)

        def y_before(L):
            return B * (L - (1 if L > 2 else 0))

        def sum_keys(dve, v, u, used, done_sem):
            dve.wait_ge(used, u + 1)
            v.tensor_reduce(O0[:, u % KT, (u // KT) * T:(u // KT) * T + T],
                            PB[SSLOT[u]].rearrange("p s t -> p t s"), AX.X, ALU.add).then_inc(done_sem, 1)

        block = ctx.enter_context(nc.Block())

        @block.sync
        def _(sp):
            xd = a["x"].rearrange("b t d -> t b d")
            for g in range(G):
                sp.dma_start(X[:, GB * g:GB * g + GB, :], xd[:, GB * g:GB * g + GB, :]).then_inc(ld_x[g], 16)
            sp.dma_start(CB[:], a["colbias"]).then_inc(ld["cb"], 16)

            def weights(dst, names, s):
                for i, n in enumerate(names):
                    sp.dma_start(dst[:, i], a[n].rearrange("(k p) n -> p k n", p=P)).then_inc(s, 16)

            weights(W0, ["L0_attn_Wk", "L0_attn_Wq", "L0_attn_Wv", "L0_attn_Wo"], ld["w0"])
            sp.dma_start(PE9[:], a["pos9"]).then_inc(ld["pe"], 16)
            weights(WX, ["wqx_t", "wkx_t", "L0_xattn_Wv"], ld["wx"])
            weights(W4, ["wk1_t", "wv1_t", "wq1_t", "wo1_t"], ld["w4"])
            for b in range(0, B, GB):
                sp.dma_start(CT[:, :, b * S:(b + GB) * S],
                             a["ctx_t"].rearrange("(k p) s -> p k s", p=P)[:, :, b * S:(b + GB) * S]
                             ).then_inc(ld["ct"], 16)
            sp.dma_start(RB[:], a["rowbias"].unsqueeze(0).broadcast_to([T, 4, D])).then_inc(ld["rows"], 16)
            sp.dma_start(BR[:], a["L0_ffn_br"].unsqueeze(0).broadcast_to([T, E])).then_inc(ld["rows"], 16)
            sp.dma_start(mki[:], a["mask_BxS2_ik1"]).then_inc(ld["masks"], 16)
            sp.dma_start(mk8[:], a["mask_keep"].bitcast(U8).rearrange("(b s) -> b s", b=B)).then_inc(ld["masks"], 16)
            for j, (s0, n) in enumerate(SJ):
                sp.dma_start(CN[0:n, j], a["ctx_1024"][:, s0:s0 + n, :].rearrange("b s d -> s b d")
                             ).then_inc(ld["cn"], 16)
            sp.dma_start(WF[:], a["wf_t"].rearrange("(k p) n -> p k n", p=P)).then_inc(ld["wf"], 16)
            sp.dma_start(WR[:], a["L0_ffn_Wr"].rearrange("(k p) n -> p k n", p=P)).then_inc(ld["wr"], 16)
            sp.wait_ge(consts, 1)
            sp.dma_start(slots_in.rearrange("(e c) d -> c e d", c=CAP),
                         zrow[:].unsqueeze(1).broadcast_to([T, E, D])).then_inc(zero_st, 16)
            sp.dma_start(zeros_d, zrow[:, 0:D // 4]).then_inc(zero_st, 16)
            sp.dma_start(ones_d, onesb[:]).then_inc(ones_st, 16)
            sp.wait_ge(masks_ready, 2)
            sp.dma_start(mask_d, mk4[:]).then_inc(mask_st, 16)
            for b in range(B):
                sp.wait_ge(k_split, b + 1)
                for i in range(3):
                    sp.dma_start(k_parts[i, :, b, :].rearrange("(k p) s -> p k s", p=P),
                                 KP[b % 2][:, i]).then_inc(k_st[b % 2], 16)
            for i in range(2):
                sp.wait_ge(k_st[i], 16 * 3 * GB)
            sp.wait_ge(x_new, B)
            sp.dma_start(W1, a["L0_ffn_W1"].rearrange("e (k p) n -> p e k n", p=P)).then_inc(ld["w1"], 16)
            sp.dma_start(W2, a["L0_ffn_W2"].rearrange("e (k p) n -> p e k n", p=P)).then_inc(ld["w2"], 16)
            sp.dma_start(WMIX, a["L1_attn_W_mix"].rearrange("(k p) n -> p k n", p=P)).then_inc(ld["wmix"], 16)
            sp.wait_ge(x_new, 2 * B)
            sp.dma_start(B2, a["L0_ffn_b2"].unsqueeze(0).broadcast_to([P, E, D])).then_inc(ld["b2"], 16)
            sp.dma_start(WA, a["L1_attn_W_aiv"].rearrange("(k p) n -> p k n", p=P)).then_inc(ld["wa"], 16)
            sp.wait_ge(scat, 16 * B)
            sp.dma_start(XN[:], slots_in.rearrange("(e c) d -> c e d", c=CAP)).then_inc(xs_ld, 16)
            for e in range(0, E, 2):
                sp.wait_ge(eo_out, e + 2)
                sp.dma_start(slots_out.rearrange("(e c) d -> c e d", c=CAP)[:, e:e + 2],
                             EO[0:CAP, e:e + 2]).then_inc(eo_st, 16)
            heads = "(h d) s -> d h s"

            def load_keys(b):
                s = b % KSLOTS
                if b < KSLOTS:
                    sp.dma_start(KS[s][KROWS:P], zero_rows(P - KROWS, S)).then_inc(ks_zero, 16)
                for r, (kp, _) in enumerate(PARTS):
                    sp.dma_start(KS[s][DK * r:DK * r + DK], k_parts[kp, :, b, :].rearrange(heads, d=DK)
                                 ).then_inc(ks_ld[s], 16)
                sp.dma_start(KS[s][ROW_MASK:ROW_MASK + 1],
                             mask_d[b:b + 1].unsqueeze(1).broadcast_to([1, H, S])).then_inc(ks_ld[s], 16)
                ones = ones_d.rearrange("a b -> (a b)")[0:S].unsqueeze(0).unsqueeze(0)
                sp.dma_start(KS[s][ROW_MAX:KROWS], ones.broadcast_to([3, H, S])).then_inc(ks_ld[s], 16)

            def zero_rows(rows, n):
                z = zeros_d.rearrange("a b -> (a b)").bitcast(BF16)[0:H * n]
                return z.rearrange("(o h n) -> o h n", o=1, h=H).broadcast_to([rows, H, n])

            sp.wait_ge(zero_st, 32)
            sp.wait_ge(ones_st, 16)
            sp.wait_ge(mask_st, 16)
            sp.wait_ge(aiv_mm, 3 * RT)
            load_keys(2)
            load_keys(3)
            sp.wait_ge(state, RT)
            load_keys(0)
            load_keys(1)
            sp.wait_ge(y_mm, 3 * B)
            sp.dma_start(QS[ROW_MASK:ROW_MASK + 1].rearrange("p h n -> p (h n)"),
                         ones_d.rearrange("a b -> (a b)")[0:H * N].unsqueeze(0)).then_inc(qs_one, 16)
            sp.dma_start(QS[ROW_MAX:P], zero_rows(P - ROW_MAX, N)).then_inc(qs_one, 16)
            for g in range(G):
                sp.wait_ge(q4_split, g + 1)
                for i in range(3):
                    sp.dma_start(q_parts[i, :, GC * g:GC * g + GC].rearrange("(k p) n -> p k n", p=P),
                                 QP[:, i]).then_inc(q_st[g], 16)
                sp.wait_ge(q_st[g], 16 * 3)
                for r, (_, qp) in enumerate(PARTS):
                    sp.dma_start(QS[DK * r:DK * r + DK, :, GC * g:GC * g + GC],
                                 q_parts[qp, :, GC * g:GC * g + GC].rearrange(heads, d=DK)
                                 ).then_inc(qs_ld[g], 16)
            for b in range(B):
                sp.wait_ge(np_out, b + 1)
                for i in range(2):
                    load_maxima(sp, b, i)
                if b >= 1 and b - 1 + KSLOTS < B:
                    sp.wait_ge(st_mm, HG * NJ * b)
                    load_keys(b - 1 + KSLOTS)
            for b in range(B):
                sp.wait_ge(x_new, B * (NBLOCKS - 1) + b + 1)
                sp.dma_start(out[b], X[:, b, :]).then_inc(out_st, 16)
            sp.wait_ge(out_st, 16 * B)
            sp.wait_ge(zero_st, 32)

        @block.gpsimd
        def _(pool):
            gp = nc.gpsimd
            link = Link(pool, pool_link)
            NQ = ALU.not_equal
            gp.memset(mhalf[:], -0.5)
            gp.memset(onesb[:], 1.0)
            link(gp.memset(identf[:], 0.0))
            link(gp.affine_select(out=identf[:], in_=identf[:], compare_op=NQ, fill=1.0, base=0,
                                  pattern=[[-1, P]], channel_multiplier=1))
            link(gp.memset(zrow[:], 0.0))
            gp.memset(onesf[:], 1.0).then_inc(consts, 1)
            link(gp.memset(M[:], 1.0))
            link(gp.affine_select(out=M[:], in_=M[:], compare_op=ALU.is_ge, fill=0.0, base=DK * 24,
                                  pattern=[[-DK, MW]], channel_multiplier=1))
            link(gp.affine_select(out=M[:], in_=M[:], compare_op=ALU.is_ge, fill=0.0,
                                  base=DK - 1 - DK * 24, pattern=[[DK, MW]], channel_multiplier=-1))
            gp.iota(negn[:], pattern=[[-1, B]], base=0, channel_multiplier=0,
                    allow_small_or_imprecise_dtypes=True).then_inc(consts, 1)
            pool.wait_ge(ld["pe"], 16)
            link(gp.tensor_tensor(DD[:], PE9[:, 1:NPOS], PE9[:, 0:B], ALU.subtract))
            gp.tensor_copy(CF[:, 0:1], PE9[:, 0:1])
            gp.tensor_copy(CF[:, 1:2], DD[:, 0:1])
            link(gp.tensor_tensor(CF[:, 2:NPOS], DD[:, 1:B], DD[:, 0:B - 1], ALU.subtract))
            gp.tensor_tensor(PEM[:], M[:].unsqueeze(1).broadcast_to([P, NPOS, MW]),
                             CF[:].unsqueeze(2).broadcast_to([P, NPOS, MW]), ALU.mult
                             ).then_inc(consts, 1)
            link(gp.memset(SELT[:], 0.0))
            sv = SELT[:].rearrange("p u (h d) -> p u h d", h=HH)
            gp.affine_select(out=sv, in_=sv, compare_op=NQ, fill=1.0, base=0,
                             pattern=[[-HH, B * KT], [-1, HH], [0, DK]], channel_multiplier=1
                             ).then_inc(consts, 1)

            def bias(L):
                if L in ROWBIAS:
                    pool.wait_ge(xn_ready, B * L + B)
                    pool.wait_ge(ld["rows"], 32)
                    gp.tensor_tensor(X[:], X[:], RB[:, ROWBIAS[L]].unsqueeze(1).broadcast_to([T, B, D]),
                                     ALU.add).then_inc(bias_added, 1)

            def rsqrt(L):
                for g in range(G):
                    pool.wait_ge(var_ready, G * L + g + 1)
                    gp.tensor_tensor(rstd[:, GB * g:GB * g + GB], ve[:, GB * g:GB * g + GB], mhalf[:],
                                     ALU.pow).then_inc(rstd_ready, 1)

            def split_key(b):
                if b >= 2:
                    pool.wait_ge(k_st[b % 2], 16 * 3 * (b // 2))
                pool.wait_ge(side_out, SIDE.index(("k", b)) + 1)
                link(gp.tensor_tensor(K32, K32, KP[b % 2][:, 0], ALU.subtract))
                link(gp.tensor_copy(KP[b % 2][:, 1], K32))
                gp.tensor_tensor(KP[b % 2][:, 2], K32, KP[b % 2][:, 1], ALU.subtract).then_inc(k_split, 1)

            rsqrt(0)
            pool.wait_ge(qkv_out, 8)
            q0, k0 = QKV[1], QKV[0]
            for i, u in enumerate(POOL_UNITS):
                s, k = UNITS[u]
                if i >= 2:
                    pool.wait_ge(prod_used, POOL_UNITS[i - 2] + 1)
                gp.tensor_tensor(PB[PSLOT[u]], k0[:, k].rearrange("p (s t) -> p s t", s=B),
                                 q0[:, k, s * T:s * T + T].unsqueeze(1).broadcast_to([P, B, T]),
                                 ALU.mult).then_inc(prod_pool, 1)
            bias(0)
            link(gp.memset(tri[:], 1.0))
            gp.affine_select(out=tri[:], in_=tri[:], compare_op=ALU.is_ge, fill=0.0, base=0,
                             pattern=[[1, T]], channel_multiplier=-1)
            link(gp.memset(selb[:], 0.0))
            link(gp.affine_select(out=selb[:], in_=selb[:], compare_op=NQ, fill=1.0, base=0,
                                  pattern=[[-1, B], [0, T]], channel_multiplier=1))
            gp.tensor_copy(identb[:], identf[:])
            gp.iota(ev8[:], pattern=[[0, B], [-1, E]], base=E, channel_multiplier=0,
                    allow_small_or_imprecise_dtypes=True).then_inc(consts, 1)
            link(gp.memset(PICK[:], 0.0))
            pv = PICK[:].rearrange("p (c w) -> p c w", c=HG)
            gp.affine_select(out=pv, in_=pv, compare_op=NQ, fill=1.0, base=0,
                             pattern=[[-32, HG], [-1, VW]], channel_multiplier=1
                             ).then_inc(consts, 1)
            pool.wait_ge(ld["masks"], 32)
            gp.tensor_scalar(mkx[:], mki[:], 0, MASKED, ALU.is_equal, ALU.mult).then_inc(masks_ready, 1)
            gp.tensor_scalar(mk4[:], mk8[:], 0, MASKED, ALU.is_equal, ALU.mult).then_inc(masks_ready, 1)
            for b in range(4):
                split_key(b)
            for i, u in enumerate(SUM_POOL):
                s, k = u // KT, u % KT
                w = PB[SSLOT[u]].rearrange("p s t -> p (s t)")
                pool.wait_ge(spread_used, u + 1)
                for n in (4 * T, 2 * T):
                    link(gp.tensor_tensor(w[:, 0:n], w[:, 0:n], w[:, n:2 * n], ALU.add))
                gp.tensor_tensor(O0[:, k, s * T:s * T + T], w[:, 0:T], w[:, T:2 * T], ALU.add
                                 ).then_inc(sum_pool, 1)
            rsqrt(1)
            pool.wait_ge(spread_used, 2 * B)
            gp.memset(V4[:, :, :, DK:VW], 1.0).then_inc(v_ones, 1)
            split_key(4)
            bias(1)
            for b in range(5, B):
                split_key(b)
            rsqrt(2)
            pool.wait_ge(slots_ready, 1)
            pool.wait_ge(zero_st, 32)
            for b in range(B):
                pool.wait_ge(xg_ready, b + 1)
                gp.indirect_dma_start(
                    slots_in, bass.IndirectOffsetOnAxis(ap=tb(11).bitcast(U32)[:, b:b + 1], axis=0),
                    XN[:, b, :], None, bounds_check=N - 1, oob_is_err=False).then_inc(scat, 16)
            pool.wait_ge(eo_st, 16 * E // 2)
            pool.wait_ge(xst_ready, 4)
            for b in range(B):
                gp.indirect_dma_start(
                    XN[:, b, :], None, slots_out,
                    bass.IndirectOffsetOnAxis(ap=tb(12).bitcast(U32)[:, b:b + 1], axis=0)
                ).then_inc(gat[b], 16)
            rsqrt(3)
            pool.wait_ge(side_mm, len(SIDE))
            gp.memset(DEC[:, :, :, 0:1], 0.0)
            gp.memset(UU[:, :, :, 0:1], 0.0)
            for t in BT:
                link(gp.memset(t, 0.0))
            gp.memset(BT[0][:, :, 0:1], 1.0 / FLOOR)
            gp.memset(BT[1][:, :, 0:1], 1.0 / FLOOR).then_inc(pads, 1)
            bias(3)
            for j in range(RT):
                pool.wait_ge(clamped, j + 1)
                if j >= 4:
                    pool.wait_ge(u_done, j - 3)
                gp.tensor_tensor(SQ[j % 4], DEC[:, j], DEC[:, j], ALU.mult).then_inc(squares, 1)
            rsqrt(4)
            bias(4)
            for b in range(B):
                i = b % 2
                pool.wait_ge(mx_out, PAIRS * (b + 1))
                if b >= 2:
                    pool.wait_ge(np_tr, b - 1)
                link(gp.tensor_copy(NP[:, i, 0], NM[:, i]))
                link(gp.tensor_tensor(NM[:, i], NM[:, i], NP[:, i, 0], ALU.subtract))
                link(gp.tensor_copy(NP[:, i, 1], NM[:, i]))
                gp.tensor_tensor(NP[:, i, 2], NM[:, i], NP[:, i, 1], ALU.subtract).then_inc(np_ready, 1)
                pool.wait_ge(np_out, b + 1)
                load_maxima(pool, b, 2)
            rsqrt(5)

        @block.scalar
        def _(act):
            sc = nc.scalar
            link = Link(act, act_link)
            done = [0]

            def xt_out(tr, first, ready):
                for g in range(G):
                    act.wait_ge(tr, first + g + 1)
                    for k in range(KT):
                        sc.activation(XT[:, k, GC * g:GC * g + GC], PS[2 * g + k][:, 0:GC], ACT.Copy
                                      ).then_inc(ready, 1)

            def side(point):
                for i in side_items(point, done):
                    kind, b = SIDE[i]
                    act.wait_ge(side_mm, i + 1)
                    if kind == "qk":
                        act.wait_ge(ld["cb"], 16)
                        sc.activation(WQK[:].rearrange("p k d -> p (k d)"), PS[6][:], ACT.Copy)
                        sc.activation(BQ16[:], PS[7][:, 0:KT], ACT.Copy, scale=1 / 16)
                        sc.activation(BQ4[:], CB[:, C_BQ1:C_BQ1 + KT], ACT.Copy, scale=1 / 4
                                      ).then_inc(side_out, 1)
                    elif kind == "k":
                        if b >= 1:
                            act.wait_ge(k_split, b)
                        if b >= 2:
                            act.wait_ge(k_st[b % 2], 16 * 3 * (b // 2))
                        for k in range(KT):
                            c = CB[:, C_BK1 + k:C_BK1 + k + 1]
                            sc.activation(K32[:, k], PS[6 + k][:, 0:S], ACT.Identity, bias=c)
                            ins = sc.activation(KP[b % 2][:, 0, k], PS[6 + k][:, 0:S], ACT.Identity, bias=c)
                        ins.then_inc(side_out, 1)
                    elif kind == "f":
                        sc.activation(fs[:, 1:2], PS[7][:, 0:1], ACT.Copy).then_inc(side_out, 1)
                    else:
                        act.wait_ge(v_ones, 1)
                        d = V4[:, NJ * b:NJ * b + NJ, :, 0:DK]
                        n0, n2 = SJ[0][1], SJ[2][1]
                        sc.activation(d[0:n0, 0:2], PS[6][0:n0, :].rearrange("p (j h d) -> p j h d", j=2, h=H),
                                      ACT.Copy)
                        sc.activation(d[0:n2, 2], PS[7][0:n2, 0:D].rearrange("p (h d) -> p h d", h=H),
                                      ACT.Copy).then_inc(side_out, 1)

            xt_out(xn_tr, 0, xt_ready)
            act.wait_ge(ld["cb"], 16)
            for i in range(12):
                w, g, m = i // 4, i // 2 % 2, i % 2
                c = (C_BK0, C_BQ0, C_BV0)[w] + m
                act.wait_ge(qkv_mm, i + 1)
                sc.activation(QKV[w][:, m, GC * g:GC * g + GC], PS[4 + i % 2][:, 0:GC], ACT.Identity,
                              bias=CB[:, c:c + 1]).then_inc(qkv_out, 1)
            side("qkv")
            for n in (4, 8, 12):
                side(f"prod{n}")
            act.wait_ge(prod_used, len(UNITS))
            for g in range(G):
                ins = sc.activation(GA[:, GB * g:GB * g + GB], PS[g][:, 0:GC].rearrange("p (s t) -> p s t", s=GB),
                                    ACT.Sigmoid, scale=0.25)
            ins.then_inc(gates, 1)
            act.wait_ge(consts, 2)
            act.wait_ge(pos_ready, 1)
            at = 0
            for n in range(1, B):
                sc.activation(R0[:, at:at + (B - n) * T], GA[:, 0:B - n].rearrange("p s t -> p (s t)"),
                              ACT.Relu, bias=negn[:, n:n + 1]).then_inc(relus, 1)
                at += (B - n) * T
            act.wait_ge(shifted, 1)
            sc.activation(AL, AL, ACT.Exp).then_inc(exp0, 1)
            side("prod16")
            xt_out(xn_tr, G, xt_ready)
            side("ln1")
            for i in range(4):
                g, m = i // 2, i % 2
                act.wait_ge(qk_mm, i + 1)
                sc.activation(QK[:, m, GC * g:GC * g + GC], PS[4 + m][:, 0:GC], ACT.Identity,
                              bias=BQ16[:, m:m + 1], scale=1 / 16).then_inc(qk_out, 1)
            for i in range(B + 1):
                if i < B:
                    act.wait_ge(sc_max, i + 1)
                    if i >= 2:
                        act.wait_ge(pt_mm, i - 1)
                    sc.activation(PX[i % 2][0:T], PS[i % 2][0:T, 0:S], ACT.Exp, bias=tb(0)[:, i:i + 1],
                                  accum_out=tb(1)[:, i:i + 1]).then_inc(sc_exp, 1)
                if i >= 1:
                    b = i - 1
                    act.wait_ge(pt_mm, b + 1)
                    if b >= 2:
                        act.wait_ge(pc_mm, b - 1)
                    n0, n2 = SJ[0][1], SJ[2][1]
                    bank = PS[2][:, 0:NJ * T].rearrange("p (j t) -> p j t", j=NJ)
                    sc.activation(PT1[b % 2][0:n0, 0:2], bank[0:n0, 0:2], ACT.Copy).then_inc(pt_out, 1)
                    sc.activation(PT1[b % 2][0:n2, 2], bank[0:n2, 2], ACT.Copy).then_inc(pt_out, 1)
                side(f"b1_{i}")
            xt_out(xn_tr, 2 * G, xt_ready)
            side("ln2")
            act.wait_ge(rt_shift, 1)
            sc.activation(tiny(3), tiny(2), ACT.Exp).then_inc(rt_exp, 1)
            side("route")
            xt_out(xs_tr, 0, xst_ready)
            for e in range(E):
                act.wait_ge(h_mm, e + 1)
                if e >= 2:
                    act.wait_ge(eo_mm, e - 1)
                for m in range(KT):
                    c = C_B1 + KT * e + m
                    ins = sc.activation(HT[e % 2][:, m], PS[4 + e % 2][:, m * CAP:(m + 1) * CAP], ACT.Relu,
                                        bias=CB[:, c:c + 1])
                ins.then_inc(h_out, 1)
            xt_out(xn_tr, 3 * G, xt_ready)
            act.wait_ge(pads, 1)
            for j in range(RT):
                for w, dst in ((0, DEC), (1, UU)):
                    i = 3 * j + w
                    act.wait_ge(aiv_mm, i + 1)
                    for g in range(G):
                        src = PS[2 * (i % 4) + g][:, 0:GC].rearrange("p (b t) -> p b t", b=GB)
                        o = dst[:, j, GB * g:GB * g + GB, 1:TP]
                        if w == 0:
                            ins = sc.activation(o, src, ACT.Sigmoid, bias=CB[:, C_DEC + j:C_DEC + j + 1])
                        else:
                            ins = sc.activation(o, src, ACT.Sigmoid)
                    ins.then_inc(sig, 1)
                if j % 4 == 3:
                    for jj in range(j - 3, j + 1):
                        act.wait_ge(squares, jj + 1)
                        sc.activation(SQ[jj % 4], SQ[jj % 4], ACT.Sqrt, scale=-1.0, bias=onesf[:, 0:1]
                                      ).then_inc(roots, 1)
            xt_out(xn_tr, 4 * G, xt_ready)
            for i in range(4):
                g, m = i // 2, i % 2
                act.wait_ge(q4_mm, i + 1)
                if i == 2:
                    act.wait_ge(q4_split, 1)
                    act.wait_ge(q_st[0], 16 * 3)
                sc.activation(QW[:, m], PS[4 + m][:, 0:GC], ACT.Identity, bias=BQ4[:, m:m + 1], scale=1 / 4)
                sc.activation(QP[:, 0, m], PS[4 + m][:, 0:GC], ACT.Identity, bias=BQ4[:, m:m + 1],
                              scale=1 / 4).then_inc(q4_out, 1)

            def exps(b, u):
                w = UNITS4 * b + u
                j, g = u // HG, u % HG
                slot = (NJ * b + j) % PSLOTS
                act.wait_ge(st_mm, w + 1)
                if NJ * b + j >= PSLOTS and g == 0:
                    act.wait_ge(pv_mm, HG * (NJ * b + j - PSLOTS + 1))
                n = SJ[j][1]
                sc.activation(P4[slot][0:n, g * HG * T:(g + 1) * HG * T], PS[4 + w % 2][0:n, 0:HG * T],
                              ACT.Exp).then_inc(st_exp, 1)

            def parts_out(b, _):
                act.wait_ge(np_tr, b + 1)
                if b >= 2:
                    act.wait_ge(nm_ld[0][b % 2], 16 * 2 * (b // 2))
                    act.wait_ge(nm_ld[1][b % 2], 16 * (b // 2))
                sc.activation(NT[b % 2][:], NPT, ACT.Copy).then_inc(np_out, 1)

            def os_evac(b, _):
                act.wait_ge(pv_mm, UNITS4 * (b + 1))
                if b >= 1:
                    act.wait_ge(os_tr, b)
                sc.activation(OS, PS[6][:, 0:HG * T], ACT.Copy).then_inc(os_out, 1)

            def ot_evac(b, _):
                act.wait_ge(on_tr, b + 1)
                if b >= 2:
                    act.wait_ge(y_mm, y_before(4) + b - 1)
                for k in range(KT):
                    c = C_BV1 + k
                    ins = sc.activation(OT[b % 2][:, k], ONT[:, k], ACT.Identity, bias=CB[:, c:c + 1])
                ins.then_inc(ot_out, 1)

            run_block4(scores=exps, parts=parts_out, os_evac=os_evac, out_tr=ot_evac)
            xt_out(xn_tr, 5 * G, xt_ready)

        @block.tensor
        def _(pe):
            mm = nc.tensor.matmul
            done = [0]

            def transposes(src, ready, first, tr):
                for g in range(G):
                    for j in range(GB):
                        b = GB * g + j
                        if first is not None:
                            pe.wait_ge(ready, first + b + 1)
                        for k in range(KT):
                            ins = nc.tensor.transpose(PS[2 * g + k][:, j * T:j * T + T],
                                                      src[:, b, k * P:(k + 1) * P], identf[0:T, 0:T])
                    ins.then_inc(tr, 1)

            def project(r, lhs, rhs, bank):
                if bank is None:
                    bank = PS[4 + r % 2]
                    if r >= 2:
                        pe.wait_ge(x_new, r - 1)
                for k in range(KT):
                    ins = mm(bank[0:T, 0:D], lhs(k), rhs(k), start=(k == 0), stop=(k == KT - 1))
                ins.then_inc(y_mm, 1)

            def side(point):
                for i in side_items(point, done):
                    kind, b = SIDE[i]
                    if i >= 1:
                        pe.wait_ge(side_out, i)
                    if kind == "qk":
                        pe.wait_ge(ld["wx"], 48)
                        pe.wait_ge(ld["cb"], 16)
                        for m in range(KT):
                            for k in range(KT):
                                mm(PS[6][:, m * D:(m + 1) * D], WX[:, 0, k, m * P:(m + 1) * P], WX[:, 1, k, :],
                                   start=(k == 0), stop=(k == KT - 1))
                        for m in range(KT):
                            for k in range(KT):
                                ins = mm(PS[7][:, m:m + 1], WX[:, 1, k, m * P:(m + 1) * P],
                                         CB[:, C_BQX + k:C_BQX + k + 1], start=(k == 0), stop=(k == KT - 1))
                    elif kind == "k":
                        pe.wait_ge(ld["w4"], 64)
                        pe.wait_ge(ld["ct"], 32)
                        for m in range(KT):
                            for k in range(KT):
                                ins = mm(PS[6 + m][:, 0:S], W4[:, 0, k, m * P:(m + 1) * P],
                                         CT[:, k, b * S:(b + 1) * S], start=(k == 0), stop=(k == KT - 1))
                    elif kind == "f":
                        pe.wait_ge(asum, 1)
                        ins = mm(PS[7][:, 0:1], onesf[:], fs[:, 3:4], start=True, stop=True)
                    else:
                        if b == 0:
                            pe.wait_ge(v_ones, 1)
                        for j, (s0, n) in enumerate(SJ):
                            o = PS[6][0:n, j * D:(j + 1) * D] if j < 2 else PS[7][0:n, 0:D]
                            for k in range(KT):
                                ins = mm(o, CT[:, k, b * S + s0:b * S + s0 + n], W4[:, 1, k, :],
                                         start=(k == 0), stop=(k == KT - 1))
                    ins.then_inc(side_mm, 1)

            pe.wait_ge(consts, 1)
            transposes(XN, xn_ready, 0, xn_tr)
            pe.wait_ge(ld["w0"], 64)
            for i in range(12):
                w, g, m = i // 4, i // 2 % 2, i % 2
                pe.wait_ge(xt_ready, KT * (g + 1))
                if i >= 2:
                    pe.wait_ge(qkv_out, i - 1)
                for k in range(KT):
                    ins = mm(PS[4 + i % 2][:, 0:GC], W0[:, w, k, m * P:(m + 1) * P], XT[:, k, GC * g:GC * g + GC],
                             start=(k == 0), stop=(k == KT - 1))
                ins.then_inc(qkv_mm, 1)
            pe.wait_ge(consts, 3)
            pe.wait_ge(qkv_out, 8)
            pe.wait_ge(xt_ready, KT * G)
            for n in range(NPOS):
                bank, c0 = (PS[2], n * T) if n < 5 else (PS[3], (n - 5) * T)
                for odd in range(2):
                    for k in range(KT):
                        x0 = 24 - (16 * odd + HH * k)
                        for c in range(4):
                            s = 2 * c + odd
                            ins = mm(bank[32 * c:32 * c + 32, c0:c0 + T], PEM[:, n, x0:x0 + 32],
                                     QKV[1][:, k, s * T:s * T + T], start=(odd == 0 and k == 0),
                                     stop=(odd == 1 and k == 1))
            ins.then_inc(cope_mm, 1)
            side("qkv")
            nd = npl = 0
            for u, (s, k) in enumerate(UNITS):
                odd, c = s % 2, s // 2
                if u in POOL_UNITS:
                    npl += 1
                    pe.wait_ge(prod_pool, npl)
                else:
                    nd += 1
                    pe.wait_ge(prod_dve, nd)
                x0 = 24 - (16 * odd + HH * k)
                for g in range(G):
                    ins = mm(PS[g][32 * c:32 * c + 32, 0:GC], M[:, x0:x0 + 32],
                             PB[PSLOT[u]][:, GB * g:GB * g + GB].rearrange("p s t -> p (s t)"),
                             start=(odd == 0 and k == 0), stop=(odd == 1 and k == 1))
                ins.then_inc(prod_used, 1)
                if u in (3, 7, 11):
                    side(f"prod{u + 1}")
            side("prod16")
            pe.wait_ge(probs0, 1)
            pe.wait_ge(consts, 4)
            pe.wait_ge(qkv_out, 12)
            for u in range(KT * B):
                if u >= 3:
                    pe.wait_ge(spread_used, u - 2)
                for g in range(G):
                    ins = mm(PS[2 * (u % 3) + g][:, 0:GC], SELT[:, u],
                             AL[:, GB * g:GB * g + GB].rearrange("p s t -> p (s t)"), start=True, stop=True)
                ins.then_inc(spread_mm, 1)
            pe.wait_ge(spread_used, KT * B)
            pe.wait_ge(sum_dve, len(SUM_DVE))
            pe.wait_ge(sum_pool, len(SUM_POOL))
            for b in range(B):
                project(b, lambda k: O0[:, k, b * T:b * T + T], lambda k: W0[:, 3, k, :], None)
            transposes(XN, xn_ready, B, xn_tr)
            side("ln1")
            pe.wait_ge(x_new, B)
            for i in range(4):
                g, m = i // 2, i % 2
                pe.wait_ge(xt_ready, KT * G + KT * (g + 1))
                if i >= 2:
                    pe.wait_ge(qk_out, i - 1)
                for k in range(KT):
                    ins = mm(PS[4 + m][:, 0:GC], WQK[:, k, m * P:(m + 1) * P], XT[:, k, GC * g:GC * g + GC],
                             start=(k == 0), stop=(k == KT - 1))
                ins.then_inc(qk_mm, 1)
            pe.wait_ge(ld["cn"], 16 * NJ)
            pe.wait_ge(masks_ready, 1)
            pe.wait_ge(consts, 5)
            pe.wait_ge(qk_out, 4)
            for i in range(B + 3):
                if i < B:
                    b = i
                    if b >= 2:
                        pe.wait_ge(sc_exp, b - 1)
                    o = PS[b % 2][0:T, 0:S]
                    for k in range(KT):
                        mm(o, QK[:, k, b * T:b * T + T], CT[:, k, b * S:(b + 1) * S], start=(k == 0), stop=False)
                    mm(o, selb[:, b, :], mkx[:], start=False, stop=True).then_inc(sc_mm, 1)
                if 1 <= i <= B:
                    b = i - 1
                    pe.wait_ge(sc_exp, b + 1)
                    if b >= 1:
                        pe.wait_ge(pt_out, 2 * b)
                    for j, (s0, n) in enumerate(SJ):
                        ins = nc.tensor.transpose(PS[2][0:n, j * T:j * T + T], PX[b % 2][0:T, s0:s0 + n],
                                                  identf[0:T, 0:T])
                    ins.then_inc(pt_mm, 1)
                if 2 <= i <= B + 1:
                    b = i - 2
                    pe.wait_ge(pt_out, 2 * (b + 1))
                    if b >= 1:
                        pe.wait_ge(pc_out, b)
                    for m in range(KT):
                        for j, (s0, n) in enumerate(SJ):
                            ins = mm(PS[3][:, m * T:m * T + T], CN[0:n, j, b, m * P:(m + 1) * P],
                                     PT1[b % 2][0:n, j], start=(j == 0), stop=(j == NJ - 1))
                    ins.then_inc(pc_mm, 1)
                if i >= 3:
                    b = i - 3
                    pe.wait_ge(pc_out, b + 1)
                    project(B + b, lambda k: PC[:, k, b * T:b * T + T], lambda k: WX[:, 2, k, :], None)
                side(f"b1_{i}")
            transposes(XN, xn_ready, 2 * B, xn_tr)
            side("ln2")
            pe.wait_ge(x_new, 2 * B)
            pe.wait_ge(xt_ready, 3 * KT * G)
            pe.wait_ge(ld["wr"], 16)
            for b in range(B):
                for k in range(KT):
                    ins = mm(PS[4][0:T, b * E:(b + 1) * E], XT[:, k, b * T:b * T + T], WR[:, k, :],
                             start=(k == 0), stop=(k == KT - 1))
            ins.then_inc(rt_mm, 1)
            pe.wait_ge(onehot, 1)
            oh = tiny(9).bitcast(BF16)
            mm(PS[5][0:T, 0:B * E], tri[:], oh[:, 0:B * E], start=True, stop=False)
            mm(PS[5][0:T, 0:B * E], onesb[0:T, 0:T], oh[:, B * E:2 * B * E], start=False, stop=True
               ).then_inc(pos_mm, 1)
            side("route")
            pe.wait_ge(xs_ld, 16)
            transposes(XN, None, None, xs_tr)
            pe.wait_ge(xst_ready, KT * G)
            pe.wait_ge(ld["w1"], 16)
            pe.wait_ge(ld["w2"], 16)
            pe.wait_ge(xg_ready, B)
            pe.wait_ge(side_out, len(SIDE))
            for i in range(E + 1):
                if i < E:
                    e = i
                    if e >= 2:
                        pe.wait_ge(h_out, e - 1)
                    for m in range(KT):
                        for k in range(KT):
                            ins = mm(PS[4 + e % 2][:, m * CAP:(m + 1) * CAP], W1[:, e, k, m * P:(m + 1) * P],
                                     XT[:, k, e * CAP:(e + 1) * CAP], start=(k == 0), stop=(k == KT - 1))
                    ins.then_inc(h_mm, 1)
                if i >= 1:
                    e = i - 1
                    pe.wait_ge(h_out, e + 1)
                    if e >= 2:
                        pe.wait_ge(eo_out, e - 1)
                    for k in range(KT):
                        ins = mm(PS[6 + e % 2][0:CAP, 0:D], HT[e % 2][:, k], W2[:, e, k, :],
                                 start=(k == 0), stop=(k == KT - 1))
                    ins.then_inc(eo_mm, 1)
            transposes(XN, xn_ready, 3 * B, xn_tr)
            pe.wait_ge(xt_ready, 4 * KT * G)
            pe.wait_ge(eo_out, E)
            pe.wait_ge(ld["wa"], 16)
            for i in range(3 * RT):
                j, w = i // 3, i % 3
                if i >= 4:
                    jp, wp = (i - 4) // 3, (i - 4) % 3
                    if wp < 2:
                        pe.wait_ge(sig, 2 * jp + wp + 1)
                    else:
                        pe.wait_ge(iv_done, jp + 1)
                for g in range(G):
                    for k in range(KT):
                        c = w * REC + j * P
                        ins = mm(PS[2 * (i % 4) + g][:, 0:GC], WA[:, k, c:c + P], XT[:, k, GC * g:GC * g + GC],
                                 start=(k == 0), stop=(k == KT - 1))
                ins.then_inc(aiv_mm, 1)
            pe.wait_ge(iv_done, RT)
            pe.wait_ge(sig, 2 * RT)
            pe.wait_ge(ld["wmix"], 16)
            for j in range(RT):
                pe.wait_ge(state, j + 1)
                for b in range(B):
                    ins = mm(PS[b][0:T, 0:D], UU[:, j, b, 1:TP], WMIX[:, j, :], start=(j == 0),
                             stop=(j == RT - 1))
                    if j == RT - 1:
                        ins.then_inc(y_mm, 1)
            pe.wait_ge(x_new, 3 * B + 4)
            transposes(XN, xn_ready, 4 * B, xn_tr)
            pe.wait_ge(x_new, 4 * B)
            for i in range(4):
                g, m = i // 2, i % 2
                pe.wait_ge(xt_ready, 4 * KT * G + KT * (g + 1))
                if i >= 2:
                    pe.wait_ge(q4_out, i - 1)
                for k in range(KT):
                    ins = mm(PS[4 + m][:, 0:GC], W4[:, 2, k, m * P:(m + 1) * P], XT[:, k, GC * g:GC * g + GC],
                             start=(k == 0), stop=(k == KT - 1))
                ins.then_inc(q4_mm, 1)
            pe.wait_ge(q4_out, 4)
            pe.wait_ge(pv_zero, 1)
            pe.wait_ge(consts, 6)
            pe.wait_ge(qs_one, 32)
            pe.wait_ge(ks_zero, 16 * KSLOTS)
            pe.wait_ge(xt_ready, 5 * KT * G)

            def maxima(b, i):
                if i == 0:
                    pe.wait_ge(ks_ld[b % KSLOTS], 16 * 8 * (b // KSLOTS + 1))
                    pe.wait_ge(qs_ld[b // GB], 16 * 6)
                w = PAIRS * b + i
                if w >= 2:
                    pe.wait_ge(mx_out, w - 1)
                for c in range(2):
                    h = 2 * i + c
                    ins = mm(PP[w % 2][0:T, c, 0:S], QS[:, h, b * T:b * T + T],
                             KS[b % KSLOTS][:, h, :], start=True, stop=True)
                ins.then_inc(mx_mm, 1)

            def parts_tr(b, _):
                pe.wait_ge(np_ready, b + 1)
                if b >= 1:
                    pe.wait_ge(np_out, b)
                if b >= 2:
                    pe.wait_ge(on_ready, b - 1)
                nc.tensor.transpose(NPT, NP[:, b % 2].rearrange("p i h -> p (i h)"), identb[0:T, 0:T]
                                    ).then_inc(np_tr, 1)

            def scores(b, u):
                j, g = u // HG, u % HG
                s0, n = SJ[j]
                w = UNITS4 * b + u
                if u == 0:
                    pe.wait_ge(nm_ld[0][b % 2], 16 * 2 * (b // 2 + 1))
                    pe.wait_ge(nm_ld[1][b % 2], 16 * (b // 2 + 1))
                if w >= 2:
                    pe.wait_ge(st_exp, w - 1)
                for c in range(HG):
                    h = HG * g + c
                    ins = mm(PS[4 + w % 2][0:n, c * T:c * T + T], KS[b % KSLOTS][:, h, s0:s0 + n],
                             QS[:, h, b * T:b * T + T], start=True, stop=True)
                ins.then_inc(st_mm, 1)

            def weighted(b, u):
                j, g = u // HG, u % HG
                n = SJ[j][1]
                if u == 0 and b >= 1:
                    pe.wait_ge(os_out, b)
                pe.wait_ge(st_exp, UNITS4 * b + u + 1)
                for c in range(4):
                    h = HG * g + c
                    ins = mm(PS[6][32 * c:32 * c + VW, g * T:g * T + T], V4[0:n, NJ * b + j, h, :],
                             P4[(NJ * b + j) % PSLOTS][0:n, h * T:h * T + T],
                             start=(u == 0), stop=(j == NJ - 1), skip_group_check=True)
                ins.then_inc(pv_mm, 1)

            def sums_tr(b, _):
                pe.wait_ge(os_out, b + 1)
                pe.wait_ge(np_out, min(B, b + 2))
                if b >= 1:
                    pe.wait_ge(x_new, 4 * B + b)
                for g in range(HG):
                    ins = mm(PS[7][0:T, g * HG * VW:(g + 1) * HG * VW], OS[:, g * T:g * T + T], PICK[:],
                             start=True, stop=True)
                ins.then_inc(os_tr, 1)

            def out_tr(b, _):
                pe.wait_ge(on_ready, b + 1)
                pe.wait_ge(np_out, min(B, b + 3))
                for k in range(KT):
                    ins = nc.tensor.transpose(ONT[:, k], zrow[:][:, k * P:(k + 1) * P], identf[0:T, 0:T])
                ins.then_inc(on_tr, 1)

            def out_mm(b, _):
                pe.wait_ge(ot_out, b + 1)
                project(4 * B + b, lambda k: OT[b % 2][:, k], lambda k: W4[:, 3, k, :], Y4)

            run_block4(maxima=maxima, parts=parts_tr, scores=scores, weighted=weighted,
                       sums_tr=sums_tr, out_tr=out_tr, out_mm=out_mm)
            transposes(XN, xn_ready, 5 * B, xn_tr)
            pe.wait_ge(wf_ready, 1)
            for b in range(B):
                pe.wait_ge(xt_ready, 5 * KT * G + KT * (b // GB + 1))
                if b < 2:
                    pe.wait_ge(x_new, 5 * B)
                project(5 * B + b, lambda k: XT[:, k, b * T:b * T + T], lambda k: WN[:, k, :], None)

        @block.vector
        def _(dve):
            v = nc.vector
            link = Link(dve, dve_link)

            def stats(L, b):
                if L == 0:
                    dve.wait_ge(ld_x[b // GB], 16)
                else:
                    dve.wait_ge(x_new, B * (L - 1) + b + 1)
                v.bn_stats(st6[:, b], X[:, b]).then_inc(stats_done, 1)

            def aggregate(L, b):
                dve.wait_ge(stats_done, B * L + b + 1)
                v.bn_aggr(mv[:, b], st6[:, b]).then_inc(aggregated, 1)

            def variance(L, g):
                sl = slice(GB * g, GB * g + GB)
                dve.wait_ge(aggregated, B * L + GB * (g + 1))
                v.tensor_scalar(ve[:, sl], mv[:, sl, 1], EPS, None, ALU.add).then_inc(var_ready, 1)

            def norm(L, g):
                dve.wait_ge(rstd_ready, G * L + g + 1)
                for b in range(GB * g, GB * g + GB):
                    v.tensor_scalar(XN[:, b], X[:, b], mv[:, b, 0:1], rstd[:, b:b + 1], ALU.subtract, ALU.mult
                                    ).then_inc(xn_ready, 1)

            def after(L, b):
                if L + 1 >= NBLOCKS:
                    return
                if b >= 1:
                    stats(L + 1, b - 1)
                if b >= 2:
                    aggregate(L + 1, b - 2)
                if b == GB + 1:
                    variance(L + 1, 0)
                if b == B - 2:
                    norm(L + 1, 0)
                if b == B - 1:
                    stats(L + 1, b)
                    aggregate(L + 1, b - 1)
                    aggregate(L + 1, b)
                    variance(L + 1, 1)
                    norm(L + 1, 1)

            def add(L, b, bank):
                dve.wait_ge(y_mm, y_before(L) + b + 1)
                if b == 0:
                    dve.wait_ge(bias_added, sum(l in ROWBIAS for l in range(L + 1)))
                v.tensor_tensor(X[:, b], X[:, b], bank[0:T, 0:D], ALU.add).then_inc(x_new, 1)
                after(L, b)

            for g in range(G):
                for b in range(GB * g, GB * g + GB):
                    stats(0, b)
                for b in range(GB * g, GB * g + GB):
                    aggregate(0, b)
                variance(0, g)
            norm(0, 0)
            norm(0, 1)
            dve.wait_ge(qkv_out, 8)
            dve.wait_ge(consts, 1)
            q0, k0, v0 = QKV[1], QKV[0], QKV[2]
            for i, u in enumerate(DVE_UNITS):
                s, k = UNITS[u]
                if i >= 3:
                    dve.wait_ge(prod_used, DVE_UNITS[i - 3] + 1)
                v.tensor_tensor(PB[PSLOT[u]], k0[:, k].rearrange("p (s t) -> p s t", s=B),
                                q0[:, k, s * T:s * T + T].unsqueeze(1).broadcast_to([P, B, T]),
                                ALU.mult).then_inc(prod_dve, 1)
            dve.wait_ge(ld["wf"], 16)
            v.tensor_reduce(fs[:, 3:4], WF[:], AX.XY, ALU.add, apply_absolute_value=True).then_inc(asum, 1)
            dve.wait_ge(gates, 1)
            for s in range(B - 2, -1, -1):
                ins = v.tensor_tensor(GA[:, s], GA[:, s], GA[:, s + 1], ALU.add)
                if s:
                    link(ins)
            ins.then_inc(pos_ready, 1)
            dve.wait_ge(pos_ready, 1)
            dve.wait_ge(cope_mm, 1)

            def coef(n, keys):
                bank, c0 = (PS[2], n * T) if n < 5 else (PS[3], (n - 5) * T)
                return bank[:, c0:c0 + T].unsqueeze(1).broadcast_to([P, keys, T])

            link(v.tensor_tensor(AC, GA, coef(1, B), ALU.mult))
            ins = v.tensor_tensor(AC, AC, coef(0, B), ALU.add)
            at, ramps = 0, []
            for n in range(1, B):
                r = R0[:, at:at + (B - n) * T].rearrange("p (s t) -> p s t", t=T)
                at += (B - n) * T
                ramps.append((n, r))
                dve.wait_ge(relus, n)
                ins = v.tensor_tensor(r, r, coef(n + 1, B - n), ALU.mult)
            link(ins)
            for n, r in ramps:
                link(v.tensor_tensor(AC[:, 0:B - n], AC[:, 0:B - n], r, ALU.add))
            dve.wait_ge(prod_used, len(UNITS))
            for g in range(G):
                ins = v.scalar_tensor_tensor(
                    out=AL[:, GB * g:GB * g + GB].rearrange("p s t -> p (s t)"), in0=PS[g][:, 0:GC], scalar=0.25,
                    in1=AC[:, GB * g:GB * g + GB].rearrange("p s t -> p (s t)"), op0=ALU.mult, op1=ALU.add)
            link(ins)
            by_token = AL.rearrange("p s t -> p t s")
            link(v.tensor_reduce(MX, by_token, AX.X, ALU.max))
            v.tensor_tensor(AL, AL, MX.unsqueeze(1).broadcast_to([P, B, T]), ALU.subtract).then_inc(shifted, 1)
            dve.wait_ge(exp0, 1)
            link(v.tensor_reduce(MX, by_token, AX.X, ALU.add))
            link(v.reciprocal(RS, MX))
            v.tensor_tensor(AL, AL, RS.unsqueeze(1).broadcast_to([P, B, T]), ALU.mult).then_inc(probs0, 1)
            dve.wait_ge(qkv_out, 12)
            nsp = 0
            for u in range(KT * B):
                s, k = u // KT, u % KT
                w = PB[SSLOT[u]]
                dve.wait_ge(spread_mm, u + 1)
                if u in SUM_POOL:
                    i = SUM_POOL.index(u)
                    if i >= 2:
                        dve.wait_ge(sum_pool, i - 1)
                elif SUM_DVE.index(u) >= 3:
                    dve.wait_ge(sum_dve, SUM_DVE.index(u) - 2)
                for g in range(G):
                    ins = v.tensor_tensor(w[:, GB * g:GB * g + GB].rearrange("p s t -> p (s t)"),
                                          PS[2 * (u % 3) + g][:, 0:GC], v0[:, k, GC * g:GC * g + GC], ALU.mult)
                ins.then_inc(spread_used, 1)
                if u - 1 in SUM_DVE and u >= 1:
                    sum_keys(dve, v, u - 1, spread_used, sum_dve)
            if KT * B - 1 in SUM_DVE:
                sum_keys(dve, v, KT * B - 1, spread_used, sum_dve)
            for b in range(B):
                add(0, b, PS[4 + b % 2])
            dve.wait_ge(side_out, SIDE.index(("f", 0)) + 1)
            link(v.tensor_scalar(fs[:, 1:2], fs[:, 1:2], 1.0 / (D * D), EPS, ALU.mult, ALU.max))
            v.tensor_scalar(fs[:, 0:1], fs[:, 1:2], 0.5, None, ALU.mult)
            link(v.tensor_scalar(fs[:, 2:3], fs[:, 1:2], -0.5, None, ALU.mult))
            v.tensor_scalar(WN[:], WF[:], fs[:, 0:1], fs[:, 1:2], ALU.is_gt, ALU.mult)
            link(v.tensor_scalar(WF[:], WF[:], fs[:, 2:3], fs[:, 1:2], ALU.is_lt, ALU.mult))
            v.tensor_tensor(WN[:], WN[:], WF[:], ALU.subtract).then_inc(wf_ready, 1)
            dve.wait_ge(bias_added, 2)
            for i in range(B + 3):
                if i < B:
                    dve.wait_ge(sc_mm, i + 1)
                    v.tensor_reduce(tb(0)[:, i:i + 1], PS[i % 2][0:T, 0:S], AX.X, ALU.max, negate=True
                                    ).then_inc(sc_max, 1)
                if 2 <= i <= B + 1:
                    b = i - 2
                    dve.wait_ge(sc_exp, b + 1)
                    v.reciprocal(tb(4)[:, b:b + 1], tb(1)[:, b:b + 1])
                    dve.wait_ge(pc_mm, b + 1)
                    v.tensor_copy(PC[:, :, b * T:b * T + T],
                                  PS[3][:, 0:KT * T].rearrange("p (k t) -> p k t", k=KT)
                                  ).then_inc(pc_out, 1)
                if i >= 3:
                    b = i - 3
                    dve.wait_ge(y_mm, B + b + 1)
                    dve.wait_ge(pc_out, b + 1)
                    v.scalar_tensor_tensor(out=X[:, b], in0=PS[4 + b % 2][0:T, 0:D], scalar=tb(4)[:, b:b + 1],
                                           in1=X[:, b], op0=ALU.mult, op1=ALU.add).then_inc(x_new, 1)
                    after(1, b)
            RL, DF, EX, OH, VM = tbe(5), tbe(2), tbe(3), tbe(6), tbe(7)
            dve.wait_ge(rt_mm, 1)
            dve.wait_ge(ld["rows"], 32)
            link(v.tensor_tensor(RL, PS[4][0:T, 0:B * E].rearrange("p (b e) -> p b e", b=B),
                                 BR[:].unsqueeze(1).broadcast_to([T, B, E]), ALU.add))
            link(v.tensor_reduce(tb(8), RL, AX.X, ALU.max))
            v.tensor_tensor(DF, RL, tb(8).unsqueeze(2).broadcast_to([T, B, E]), ALU.subtract
                            ).then_inc(rt_shift, 1)
            dve.wait_ge(rt_shift, 1)
            link(v.tensor_scalar(OH, DF, 0.0, None, ALU.is_ge))
            link(v.tensor_tensor(OH, OH, ev8[:], ALU.mult))
            link(v.tensor_reduce(tb(8), OH, AX.X, ALU.max))
            link(v.tensor_tensor(OH, OH, tb(8).unsqueeze(2).broadcast_to([T, B, E]), ALU.is_equal))
            oh = tiny(9).bitcast(BF16).rearrange("p (c b e) -> p c b e", c=2, b=B)
            v.memset(oh[:, 1, 0], 0.0)
            link(v.tensor_copy(oh[:, 0], OH))
            for b in range(1, B):
                ins = v.tensor_tensor(oh[:, 1, b], oh[:, 1, b - 1], oh[:, 0, b - 1], ALU.add)
                if b < B - 1:
                    link(ins)
            ins.then_inc(onehot, 1)
            GATE, POS, KEEP, SL = tb(1), tb(4), tb(10), tb(13)
            dve.wait_ge(rt_exp, 1)
            link(v.tensor_reduce(GATE, EX, AX.X, ALU.add))
            link(v.reciprocal(GATE, GATE))
            dve.wait_ge(pos_mm, 1)
            link(v.tensor_tensor(VM, OH, PS[5][0:T, 0:B * E].rearrange("p (b e) -> p b e", b=B), ALU.mult))
            link(v.tensor_reduce(POS, VM, AX.X, ALU.add))
            v.tensor_scalar(KEEP, POS, float(CAP), None, ALU.is_lt)
            v.tensor_scalar(SL, tb(8), -float(CAP), float(CAP * E), ALU.mult, ALU.add)
            link(v.tensor_scalar(tb(2), POS, float(CAP), float(4 * N), ALU.is_ge, ALU.mult))
            link(v.tensor_tensor(SL, SL, POS, ALU.add))
            v.tensor_tensor(tb(11).bitcast(I32), SL, tb(2), ALU.add)
            v.tensor_tensor(tb(12).bitcast(I32), SL, KEEP, ALU.mult).then_inc(slots_ready, 1)
            link(v.tensor_tensor(GATE, GATE, KEEP, ALU.mult))
            for b in range(B):
                v.tensor_scalar(XN[:, b], XN[:, b], GATE[:, b:b + 1], None, ALU.mult).then_inc(xg_ready, 1)
            dve.wait_ge(ld["b2"], 16)
            for e in range(E):
                dve.wait_ge(eo_mm, e + 1)
                v.tensor_tensor(EO[0:CAP, e], PS[6 + e % 2][0:CAP, 0:D], B2[0:CAP, e], ALU.add
                                ).then_inc(eo_out, 1)
            for b in range(B):
                dve.wait_ge(gat[b], 16)
                v.scalar_tensor_tensor(out=X[:, b], in0=XN[:, b], scalar=GATE[:, b:b + 1], in1=X[:, b],
                                       op0=ALU.mult, op1=ALU.add).then_inc(x_new, 1)
                after(2, b)
            def flat(t):
                return t.rearrange("p b t -> p (b t)")

            def inputs(j):
                dve.wait_ge(roots, j + 1)
                v.scalar_tensor_tensor(out=flat(UU[:, j]), in0=flat(SQ[j % 4]), scalar=1e-4, in1=flat(UU[:, j]),
                                       op0=ALU.max, op1=ALU.mult).then_inc(u_done, 1)
                dve.wait_ge(u_done, j + 1)
                v.tensor_tensor_scan(flat(UU[:, j]), flat(DEC[:, j]), flat(UU[:, j]), 0.0, ALU.mult, ALU.add
                                     ).then_inc(state, 1)

            dve.wait_ge(pads, 1)
            for j in range(RT):
                a_t = DEC[:, j, :, 1:TP]
                bt = BT[j % 2]
                dve.wait_ge(sig, 2 * j + 1)
                v.tensor_scalar(a_t, a_t, FLOOR, 1.0, ALU.max, ALU.min).then_inc(clamped, 1)
                dve.wait_ge(clamped, j + 1)
                v.tensor_scalar(bt[:, :, 1 + CHUNK:2 + CHUNK], DEC[:, j, :, 1 + CHUNK:2 + CHUNK],
                                1.0 / FLOOR, None, ALU.mult).then_inc(reset64, 1)
                dve.wait_ge(reset64, j + 1)
                v.tensor_tensor_scan(flat(CD), flat(DEC[:, j]), flat(bt), 0.0, ALU.mult, ALU.max
                                     ).then_inc(cdec, 1)
                dve.wait_ge(sig, 2 * j + 2)
                dve.wait_ge(aiv_mm, 3 * j + 3)
                for g in range(G):
                    o = UU[:, j, GB * g:GB * g + GB, 1:TP]
                    src = PS[2 * ((3 * j + 2) % 4) + g][:, 0:GC].rearrange("p (b t) -> p b t", b=GB)
                    ins = v.tensor_tensor(o, o, src, ALU.mult)
                ins.then_inc(iv_done, 1)
                dve.wait_ge(iv_done, j + 1)
                dve.wait_ge(cdec, j + 1)
                link(v.scalar_tensor_tensor(out=flat(UU[:, j]), in0=flat(CD), scalar=1.0, in1=flat(UU[:, j]),
                                            op0=ALU.min, op1=ALU.mult))
                if j >= 4:
                    inputs(j - 4)
            for j in range(RT - 4, RT):
                inputs(j)
            for b in range(B):
                add(3, b, PS[b])
            dve.wait_ge(x_new, 4 * B)
            for g in range(G):
                dve.wait_ge(q4_out, 2 * g + 2)
                link(v.tensor_tensor(QW, QW, QP[:, 0], ALU.subtract))
                link(v.tensor_copy(QP[:, 1], QW))
                v.tensor_tensor(QP[:, 2], QW, QP[:, 1], ALU.subtract).then_inc(q4_split, 1)
            v.memset(PS[6], 0.0).then_inc(pv_zero, 1)

            def row_max(b, i):
                w = PAIRS * b + i
                dve.wait_ge(mx_mm, w + 1)
                if i == 0 and b >= 2:
                    dve.wait_ge(np_ready, b - 1)
                v.tensor_reduce(NM[:, b % 2, 2 * i:2 * i + 2], PP[w % 2][0:T, :, 0:S], AX.X, ALU.max, negate=True
                                ).then_inc(mx_out, 1)

            def normalise(b, _):
                dve.wait_ge(os_tr, b + 1)
                if b >= 1:
                    dve.wait_ge(on_tr, b)
                o = PS[7][0:T, 0:H * VW].rearrange("p (h w) -> p h w", h=H)
                link(v.reciprocal(RC4[:], o[:, :, DK]))
                v.tensor_tensor(ON, o[:, :, 0:DK], RC4[:].unsqueeze(2).broadcast_to([T, H, DK]), ALU.mult
                                ).then_inc(on_ready, 1)

            run_block4(maxima=row_max, normalise=normalise, add=lambda b, _: add(4, b, Y4))
            for b in range(B):
                add(5, b, PS[4 + b % 2])


_OUT = (B, T, D)


def kernel(**inputs):
    import concourse.bacc as bacc
    from concourse.bass_utils import run_bass_kernel_spmd

    nc = bacc.Bacc("TRN2", target_bir_lowering=False, num_devices=1)
    x = {n: np.asarray(v) for n, v in inputs.items()}

    def cols(v):
        return v.reshape(-1, P).T

    laid = {n: x[n] for n in ("x", "ctx_1024", "mask_BxS2_ik1", "L0_attn_Wq", "L0_attn_Wk", "L0_attn_Wv",
                              "L0_attn_Wo", "L0_xattn_Wv", "L0_ffn_Wr", "L0_ffn_br", "L0_ffn_W1", "L0_ffn_W2",
                              "L0_ffn_b2", "L1_attn_W_aiv", "L1_attn_W_mix")}
    laid["mask_keep"] = x["mask_BxS2_bk0"].reshape(-1).view(np.uint32)
    laid["ctx_t"] = x["ctx_1024"].transpose(2, 0, 1).reshape(D, B * S)
    laid["wqx_t"] = x["L0_xattn_Wq"].T
    laid["wkx_t"] = x["L0_xattn_Wk"].T
    laid["wk1_t"] = x["L1_xattn_Wk"].T
    laid["wv1_t"] = x["L1_xattn_Wv"].T
    laid["wq1_t"] = x["L1_xattn_Wq"].T
    laid["wo1_t"] = x["L1_xattn_Wo"].T
    laid["wf_t"] = x["L1_ffn_weight"].T
    laid["pos9"] = np.concatenate([x["L0_attn_pos_emb"][0][:, :NPOS]] * HH, axis=0)
    laid["colbias"] = np.concatenate([cols(x[n]) for n in (
        "L0_attn_bq", "L0_attn_bk", "L0_attn_bv", "L0_xattn_bq", "L1_xattn_bk", "L1_xattn_bq", "L1_xattn_bv",
        "L1_attn_decay_bias", "L0_ffn_b1")], axis=1)
    laid["rowbias"] = np.stack([x[n] for n in ("L0_attn_bo", "L0_xattn_bv", "L1_attn_b_mix", "L1_xattn_bo")])
    arrays, aps = {}, {}
    for n, v in laid.items():
        v = np.ascontiguousarray(v)
        arrays["in_" + n] = v
        aps[n] = nc.dram_tensor("in_" + n, v.shape, mybir.dt.from_np(v.dtype), kind="ExternalInput").ap()
    out = nc.dram_tensor("out_x", _OUT, F32, kind="ExternalOutput").ap()
    build(nc, aps, out)
    r = run_bass_kernel_spmd(nc, [arrays], core_ids=[0])
    return r.results[0]["out_x"]
```

```python
from contextlib import ExitStack

import numpy as np

import concourse.bass as bass
from concourse import mybir

F32 = mybir.dt.float32
BF16 = mybir.dt.bfloat16
I32 = mybir.dt.int32
U32 = mybir.dt.uint32
U8 = mybir.dt.uint8
ALU = mybir.AluOpType
ACT = mybir.ActivationFunctionType
AX = mybir.AxisListType

B, T, D = 8, 100, 256
S = 361
H, DK = 16, 16
E = 8
N = B * T
CAP = N // E
P = 128
KT = D // P
HH = P // DK
G = 2
GB = B // G
GC = GB * T
EPS = 1e-5
MASKED = -1e30
REC = 1024
RT = REC // P
CHUNK = 64
TP = T + 1
FLOOR = 1e-10
NPOS = B + 1
SJ = [(0, 121), (121, 121), (242, 119)]
NJ = len(SJ)
PARTS = [(0, 0), (0, 1), (0, 2), (1, 0), (1, 1), (2, 0)]
ROW_MASK = len(PARTS) * DK
ROW_MAX = ROW_MASK + 1
KROWS = ROW_MAX + 3
HG = 4
VW = DK + 1
KSLOTS = 4
PSLOTS = 4
C_BQ0, C_BK0, C_BV0, C_BQX, C_BK1, C_BQ1, C_BV1, C_DEC, C_B1 = 0, 2, 4, 6, 8, 10, 12, 14, 22
NCB = C_B1 + 2 * E
R_BO0, R_BVX, R_BMIX, R_BO1 = range(4)
ROWBIAS = {0: R_BO0, 1: R_BVX, 3: R_BMIX, 4: R_BO1}
NBLOCKS = 6


def build(nc, a, out):
    ctx = ExitStack()
    with ctx:
        def sb(name, shape, dt=F32):
            return ctx.enter_context(nc.sbuf_tensor(name, shape, dt))

        def sem(name):
            return ctx.enter_context(nc.semaphore(name))

        def dram(name, shape, dt=F32):
            return nc.dram_tensor(name, shape, dt, kind="Internal").ap()

        PP = [ctx.enter_context(nc.psum_tensor(f"banks{i}", [P, 2, 512], F32)) for i in range(4)]
        PS = [PP[i // 2][:, i % 2] for i in range(8)]

        X = sb("X", [T, B, D])
        XN = sb("XN", [T, B, D])
        XT = sb("XT", [P, KT, N])
        identf = sb("identf", [P, P])
        identb = sb("identb", [P, P], BF16)
        onesf = sb("onesf", [P, P])
        onesb = sb("onesb", [P, P], BF16)
        tri = sb("tri", [T, T], BF16)
        selb = sb("selb", [B, B, T], BF16)
        negn = sb("negn", [P, B])
        PICK = sb("PICK", [P, HG * VW])
        ev8 = sb("ev8", [T, B, E])
        mhalf = sb("mhalf", [T, GB])
        ve = sb("ve", [T, B])
        zrow = sb("zrow", [T, D])
        CB = sb("CB", [P, NCB])
        RB = sb("RB", [T, 4, D])
        BR = sb("BR", [T, E])
        BQ16 = sb("BQ16", [P, KT])
        BQ4 = sb("BQ4", [P, KT])
        PE9 = sb("PE9", [P, NPOS])
        DD = sb("DD", [P, B])
        CF = sb("CF", [P, NPOS])
        MW = 24 + HH + 24
        M = sb("M", [P, MW])
        PEM = sb("PEM", [P, NPOS, MW])
        SELT = sb("SELT", [P, B * KT, P])
        W0 = sb("W0", [P, 4, KT, D])
        WMIX = W0[:].rearrange("p a k d -> p (a k) d")
        WX = sb("WX", [P, 3, KT, D])
        WQK = sb("WQK", [P, KT, D])
        W4 = sb("W4", [P, 4, KT, D])
        WR = sb("WR", [P, KT, E])
        WF = sb("WF", [P, KT, D])
        WN = sb("WN", [P, KT, D])
        fs = sb("fs", [P, 4])
        st6 = sb("st6", [T, B, 6])
        mv = sb("mv", [T, B, 2])
        rstd = sb("rstd", [T, B])
        mki = sb("mki", [B, S], I32)
        mkx = sb("mkx", [B, S], BF16)
        mk8 = sb("mk8", [B, S], U8)
        mk4 = sb("mk4", [B, S], BF16)
        CT = sb("CT", [P, KT, B * S])
        small = sb("small", [T, 14 * B * E])

        RA = sb("RA", [P, 8200])
        RBG = sb("RBG", [P, 2 * 3 * REC])
        RC = sb("RC", [P, 6500])
        RV = sb("RV", [P, B * NJ * H * VW])

        def part(region, at, *dims, dt=F32):
            n = int(np.prod(dims))
            words = n if dt != BF16 else (n + 1) // 2
            v = region[:, at:at + words]
            if dt != F32:
                v = v.bitcast(dt)
            names = "abcd"[:len(dims)]
            if len(dims) > 1:
                v = v.rearrange("p (" + " ".join(names) + ") -> p " + " ".join(names),
                                **dict(zip(names, dims)))
            return v

        R0 = part(RA, 0, 28 * T)
        O0 = part(RA, 2800, KT, N)
        K32 = [part(RA, 4400 + 3000 * i, KT, S) for i in range(2)]
        KP = [part(RA, 5124 + 1083 * i, 3, KT, S, dt=BF16) for i in range(2)]
        for r, at in ((SELT[:].rearrange("p a b -> p (a b)"), 0), (RC, 4600)):
            K32.append(part(r, at, KT, S))
            KP.append(part(r, at + KT * S, 3, KT, S, dt=BF16))
        PB = [part(RC, 800 * i, B, T) for i in range(5)]
        GA = part(RC, 4000, B, T)
        AC = part(RC, 4800, B, T)
        AL = part(RC, 5600, B, T)
        MX = part(RC, 6400, T)
        RS = part(RA, 7290, T)
        QKV = [part(RV, 1600 * i, KT, N) for i in range(3)]
        CN = part(RBG, 0, NJ, B, D)
        QK = part(RC, 0, KT, N)
        PX = [part(RC, 1600 + 364 * i, S) for i in range(2)]
        PT1 = [part(RC, 2400 + 300 * i, NJ, T) for i in range(2)]
        PC = part(RC, 3000, KT, N)
        W1 = part(RA, 0, E, KT, D)
        W2 = part(RA, 4096, E, KT, D)
        HT = [part(RC, 200 * i, KT, CAP) for i in range(2)]
        EO = part(RC, 400, E, D)
        B2 = part(RC, 2448, E, D)
        WA = part(RBG, 0, KT, 3 * REC)
        DEC = part(RA, 0, RT, B, TP)
        UU = part(RC, 0, RT, B, TP)
        CTF = CT[:].rearrange("p k s -> p (k s)")
        SQ = [part(CTF, 808 * i, B, TP) for i in range(4)]
        CD = part(CTF, 808 * 4, B, TP)
        BT = [part(CTF, 808 * (5 + i), B, TP) for i in range(2)]
        V4 = part(RV, 0, B * NJ, H, VW)
        KS = [part(r, H * S // 2 * i, H, S, dt=BF16) for r in (RA, RBG) for i in range(2)]
        QS = part(RC, 0, H, N, dt=BF16)
        P4 = [part(CTF, 1600 * i, H * T) for i in range(3)] + [
            part(SELT[:].rearrange("p a b -> p (a b)"), 0, H * T)]
        QW = part(CTF, 4800, KT, GC)
        QP = part(WX[:].rearrange("p a k d -> p (a k d)"), 0, 3, KT, GC, dt=BF16)
        NM = sb("NM", [T, 2, H])
        NP = sb("NP", [T, 2, 3, H], BF16)
        NT = [sb(f"NT{i}", [3 * H, T], BF16) for i in range(2)]
        ONT = PS[7][:, 0:KT * T].rearrange("p (k t) -> p k t", k=KT)
        Y4 = PS[7][:, KT * T:KT * T + D]
        NPT = PS[7][0:3 * H, 460:460 + T // 2].bitcast(BF16)
        OS = part(WQK[:].rearrange("p k d -> p (k d)"), 0, HG * T)
        RC4 = sb("RC4", [T, H])
        ON = zrow[:].rearrange("p (h d) -> p h d", h=H)
        OT = [part(PEM[:].rearrange("p n x -> p (n x)"), KT * T * i, KT, T) for i in range(2)]

        def tiny(i, n=B * E):
            return small[:, i * B * E:i * B * E + n]

        def tbe(i):
            return tiny(i).rearrange("p (b e) -> p b e", b=B)

        def tb(i):
            return tiny(i, B)

        slots_in = dram("slots_in", [N, D])
        slots_out = dram("slots_out", [N, D])
        k_parts = dram("k_parts", [3, D, B, S], BF16)
        q_parts = dram("q_parts", [3, D, N], BF16)
        mask_d = dram("mask_d", [B, S], BF16)
        ones_d = dram("ones_d", [P, P], BF16)
        zeros_d = dram("zeros_d", [T, D // 4])

        ld_x = [sem(f"ld_x{g}") for g in range(G)]
        ld = {n: sem("ld_" + n) for n in ("cb", "w0", "pe", "ct", "cn", "wx", "w4", "rows", "masks",
                                          "wr", "wf", "w1", "w2", "b2", "wa", "wmix")}
        zero_st = sem("zero_st")
        ones_st = sem("ones_st")
        mask_st = sem("mask_st")
        k_st = [sem(f"k_st{i}") for i in range(4)]
        scat = sem("scat")
        xs_ld = [sem(f"xs_ld{g}") for g in range(G)]
        eo_st = sem("eo_st")
        gat = [sem(f"gat{b}") for b in range(B)]
        q_st = [[sem(f"q_st{g}{i}") for i in range(3)] for g in range(G)]
        qs_ld = [sem(f"qs_ld{g}") for g in range(G)]
        qs_one = sem("qs_one")
        ks_zero = sem("ks_zero")
        ks_ld = [sem(f"ks_ld{i}") for i in range(KSLOTS)]
        nm_ld = [[sem(f"nm_{q}{i}") for i in range(2)] for q in ("sp", "pool")]
        out_st = sem("out_st")
        consts = sem("consts")
        dve_link = sem("dve_link")
        act_link = sem("act_link")
        pool_link = sem("pool_link")
        stats_done = sem("stats_done")
        aggregated = sem("aggregated")
        var_ready = sem("var_ready")
        rstd_ready = sem("rstd_ready")
        xn_ready = sem("xn_ready")
        xn_tr = sem("xn_tr")
        xt_ready = sem("xt_ready")
        bias_added = sem("bias_added")
        y_mm = sem("y_mm")
        x_new = sem("x_new")
        side_mm = sem("side_mm")
        side_out = sem("side_out")
        qkv_mm = sem("qkv_mm")
        qkv_out = sem("qkv_out")
        cope_mm = sem("cope_mm")
        prod_dve = sem("prod_dve")
        prod_pool = sem("prod_pool")
        prod_used = sem("prod_used")
        gates = sem("gates")
        pos_ready = sem("pos_ready")
        relus = sem("relus")
        shifted = sem("shifted")
        exp0 = sem("exp0")
        probs0 = sem("probs0")
        spread_mm = sem("spread_mm")
        spread_used = sem("spread_used")
        sum_dve = sem("sum_dve")
        sum_pool = sem("sum_pool")
        k_split = sem("k_split")
        v_ones = sem("v_ones")
        masks_ready = sem("masks_ready")
        wf_ready = sem("wf_ready")
        asum = sem("asum")
        qk_mm = sem("qk_mm")
        qk_out = sem("qk_out")
        sc_mm = sem("sc_mm")
        sc_max = sem("sc_max")
        sc_exp = sem("sc_exp")
        pt_mm = sem("pt_mm")
        pt_out = sem("pt_out")
        pc_mm = sem("pc_mm")
        pc_out = sem("pc_out")
        rt_mm = sem("rt_mm")
        rt_shift = sem("rt_shift")
        rt_exp = sem("rt_exp")
        onehot = sem("onehot")
        pos_mm = sem("pos_mm")
        xg_ready = sem("xg_ready")
        slots_ready = sem("slots_ready")
        xs_tr = sem("xs_tr")
        xst_ready = sem("xst_ready")
        h_mm = sem("h_mm")
        h_out = sem("h_out")
        eo_mm = sem("eo_mm")
        eo_out = sem("eo_out")
        aiv_mm = sem("aiv_mm")
        sig = sem("sig")
        clamped = sem("clamped")
        iv_done = sem("iv_done")
        squares = sem("squares")
        roots = sem("roots")
        u_done = sem("u_done")
        state = sem("state")
        pads = sem("pads")
        reset64 = sem("reset64")
        cdec = sem("cdec")
        q4_mm = sem("q4_mm")
        q4_out = sem("q4_out")
        q4_split = sem("q4_split")
        q4_split1 = sem("q4_split1")
        mx_mm = sem("mx_mm")
        mx_out = sem("mx_out")
        np_ready = sem("np_ready")
        np_tr = sem("np_tr")
        np_out = sem("np_out")
        st_mm = sem("st_mm")
        st_exp = sem("st_exp")
        pv_mm = sem("pv_mm")
        pv_zero = sem("pv_zero")
        os_out = sem("os_out")
        os_tr = sem("os_tr")
        on_ready = sem("on_ready")
        on_tr = sem("on_tr")
        ot_out = sem("ot_out")

        class Link:

            def __init__(self, eng, semaphore):
                self.eng, self.sem, self.n = eng, semaphore, 0

            def __call__(self, ins):
                self.n += 1
                ins.then_inc(self.sem, 1)
                self.eng.wait_ge(self.sem, self.n)

        SIDE = ([("qk", 0)] + [("k", b) for b in range(6)]
                + [("v", 0), ("v", 1), ("k", 6), ("k", 7)] + [("v", b) for b in range(2, B)] + [("f", 0)])
        SIDE_AT = {"cope": 3, "ln1": 4, "b1_0": 5, "b1_2": 6, "b1_4": 7, "b1_6": 8, "ln2": 9,
                   "router": 10, "route": 13, "gather": 18}
        SIDE_LOW = [1, 14, 16]

        def side_bank(i):
            return 4 if i in SIDE_LOW else 6

        def side_before(i):
            same = [j for j in range(i) if side_bank(j) == side_bank(i)]
            return same[-1] + 1 if same else 0

        def side_items(point, done):
            n = SIDE_AT.get(point, 0)
            items = list(range(done[0], n))
            done[0] = max(done[0], n)
            return items

        UNITS = [(s, k) for odd in range(2) for k in range(KT) for s in range(odd, B, 2)]
        POOL_UNITS = [u for u in range(len(UNITS)) if u % 4 == 3]
        DVE_UNITS = [u for u in range(len(UNITS)) if u % 4 != 3]
        PSLOT = {u: i % 3 for i, u in enumerate(DVE_UNITS)} | {u: 3 + i % 2 for i, u in enumerate(POOL_UNITS)}
        SUM_POOL = [u for u in range(2 * B) if u % 3 == 1]
        SUM_DVE = [u for u in range(2 * B) if u % 3 != 1]
        SSLOT = {u: i % 3 for i, u in enumerate(SUM_DVE)} | {u: 3 + i % 2 for i, u in enumerate(SUM_POOL)}

        PAIRS = H // 2
        UNITS4 = HG * NJ
        TICKS = 2 * PAIRS
        PLAN = ([("maxima", 2 * i, i) for i in range(PAIRS)]
                + [("parts", 21, 0)]
                + [("scores", 28 + TICKS * u // UNITS4, u) for u in range(UNITS4)]
                + [("weighted", max(35 + u // 2, 32 + TICKS * u // UNITS4), u) for u in range(UNITS4)]
                + [("os_evac", 46, 0), ("sums_tr", 49, 0), ("normalise", 49, 0), ("out_tr", 56, 0),
                   ("out_mm", 58, 0), ("add", 59, 0)])
        PLAN_END = TICKS * (B - 1) + 60
        ORDER = ("parts", "sums_tr", "normalise", "out_tr", "out_mm", "maxima", "scores", "weighted",
                 "os_evac", "add")

        def run_block4(**own):
            for tick in range(PLAN_END):
                for name in ORDER:
                    for n, at, x in PLAN:
                        b = (tick - at) // TICKS
                        if n == name and name in own and (tick - at) % TICKS == 0 and 0 <= b < B:
                            own[name](b, x)

        def load_queries(queue, g, i):
            queue.wait_ge(q_st[g][i], 16)
            for r, (_, qp) in enumerate(PARTS):
                if qp == i:
                    queue.dma_start(QS[DK * r:DK * r + DK, :, GC * g:GC * g + GC],
                                    q_parts[qp, :, GC * g:GC * g + GC].rearrange("(h d) s -> d h s", d=DK)
                                    ).then_inc(qs_ld[g], 16)

        def load_maxima(queue, b, i):
            queue.dma_start(QS[ROW_MAX + i:ROW_MAX + i + 1, :, b * T:b * T + T],
                            NT[b % 2][H * i:H * i + H]).then_inc(nm_ld[i == 2][b % 2], 16)

        def k_buffer(b):
            return b % 2 if b < 6 else b - 4

        def aiv_pair(i):
            return (i + 2) % 4

        def y_before(L):
            return B * (L - (1 if L > 2 else 0))

        def sum_keys(dve, v, u, used, done_sem):
            dve.wait_ge(used, u + 1)
            v.tensor_reduce(O0[:, u % KT, (u // KT) * T:(u // KT) * T + T],
                            PB[SSLOT[u]].rearrange("p s t -> p t s"), AX.X, ALU.add).then_inc(done_sem, 1)

        block = ctx.enter_context(nc.Block())

        @block.sync
        def _(sp):
            xd = a["x"].rearrange("b t d -> t b d")
            for g in range(G):
                sp.dma_start(X[:, GB * g:GB * g + GB, :], xd[:, GB * g:GB * g + GB, :]).then_inc(ld_x[g], 16)
            sp.dma_start(CB[:], a["colbias"]).then_inc(ld["cb"], 16)

            def weights(dst, names, s):
                for i, n in enumerate(names):
                    sp.dma_start(dst[:, i], a[n].rearrange("(k p) n -> p k n", p=P)).then_inc(s, 16)

            weights(W0, ["L0_attn_Wk", "L0_attn_Wq", "L0_attn_Wv", "L0_attn_Wo"], ld["w0"])
            sp.dma_start(PE9[:], a["pos9"]).then_inc(ld["pe"], 16)
            weights(WX, ["wqx_t", "wkx_t", "L0_xattn_Wv"], ld["wx"])
            weights(W4, ["wk1_t", "wv1_t", "wq1_t", "wo1_t"], ld["w4"])
            for b in range(0, B, GB):
                sp.dma_start(CT[:, :, b * S:(b + GB) * S],
                             a["ctx_t"].rearrange("(k p) s -> p k s", p=P)[:, :, b * S:(b + GB) * S]
                             ).then_inc(ld["ct"], 16)
            sp.dma_start(RB[:], a["rowbias"].unsqueeze(0).broadcast_to([T, 4, D])).then_inc(ld["rows"], 16)
            sp.dma_start(BR[:], a["L0_ffn_br"].unsqueeze(0).broadcast_to([T, E])).then_inc(ld["rows"], 16)
            sp.dma_start(mki[:], a["mask_BxS2_ik1"]).then_inc(ld["masks"], 16)
            sp.dma_start(mk8[:], a["mask_keep"].bitcast(U8).rearrange("(b s) -> b s", b=B)).then_inc(ld["masks"], 16)
            for j, (s0, n) in enumerate(SJ):
                sp.dma_start(CN[0:n, j], a["ctx_1024"][:, s0:s0 + n, :].rearrange("b s d -> s b d")
                             ).then_inc(ld["cn"], 16)
            sp.dma_start(WF[:], a["wf_t"].rearrange("(k p) n -> p k n", p=P)).then_inc(ld["wf"], 16)
            sp.dma_start(WR[:], a["L0_ffn_Wr"].rearrange("(k p) n -> p k n", p=P)).then_inc(ld["wr"], 16)
            sp.wait_ge(consts, 1)
            sp.dma_start(slots_in.rearrange("(e c) d -> c e d", c=CAP),
                         zrow[:].unsqueeze(1).broadcast_to([T, E, D])).then_inc(zero_st, 16)
            sp.dma_start(zeros_d, zrow[:, 0:D // 4]).then_inc(zero_st, 16)
            sp.dma_start(ones_d, onesb[:]).then_inc(ones_st, 16)
            sp.wait_ge(masks_ready, 2)
            sp.dma_start(mask_d, mk4[:]).then_inc(mask_st, 16)
            def store_keys(b):
                sp.wait_ge(k_split, b + 1)
                for i in range(3):
                    sp.dma_start(k_parts[i, :, b, :].rearrange("(k p) s -> p k s", p=P),
                                 KP[k_buffer(b)][:, i]).then_inc(k_st[k_buffer(b)], 16)

            for b in range(6):
                store_keys(b)
            for i in range(2):
                sp.wait_ge(k_st[i], 16 * 3 * 3)
            sp.wait_ge(x_new, B)
            sp.dma_start(W1, a["L0_ffn_W1"].rearrange("e (k p) n -> p e k n", p=P)).then_inc(ld["w1"], 16)
            sp.dma_start(W2, a["L0_ffn_W2"].rearrange("e (k p) n -> p e k n", p=P)).then_inc(ld["w2"], 16)
            sp.dma_start(WMIX, a["L1_attn_W_mix"].rearrange("(k p) n -> p k n", p=P)).then_inc(ld["wmix"], 16)
            sp.wait_ge(x_new, 2 * B)
            sp.dma_start(B2, a["L0_ffn_b2"].unsqueeze(0).broadcast_to([P, E, D])).then_inc(ld["b2"], 16)
            sp.dma_start(WA, a["L1_attn_W_aiv"].rearrange("(k p) n -> p k n", p=P)).then_inc(ld["wa"], 16)
            sp.wait_ge(scat, 16 * B)
            for g in range(G):
                sp.dma_start(XN[:, GB * g:GB * g + GB],
                             slots_in.rearrange("(e c) d -> c e d", c=CAP)[:, GB * g:GB * g + GB]
                             ).then_inc(xs_ld[g], 16)
            store_keys(6)
            for e in range(0, E, 2):
                if e == 2:
                    store_keys(7)
                sp.wait_ge(eo_out, e + 2)
                sp.dma_start(slots_out.rearrange("(e c) d -> c e d", c=CAP)[:, e:e + 2],
                             EO[0:CAP, e:e + 2]).then_inc(eo_st, 16)
            heads = "(h d) s -> d h s"

            def load_keys(b):
                s = b % KSLOTS
                if b < KSLOTS:
                    sp.dma_start(KS[s][KROWS:P], zero_rows(P - KROWS, S)).then_inc(ks_zero, 16)
                for r, (kp, _) in enumerate(PARTS):
                    sp.dma_start(KS[s][DK * r:DK * r + DK], k_parts[kp, :, b, :].rearrange(heads, d=DK)
                                 ).then_inc(ks_ld[s], 16)
                sp.dma_start(KS[s][ROW_MASK:ROW_MASK + 1],
                             mask_d[b:b + 1].unsqueeze(1).broadcast_to([1, H, S])).then_inc(ks_ld[s], 16)
                ones = ones_d.rearrange("a b -> (a b)")[0:S].unsqueeze(0).unsqueeze(0)
                sp.dma_start(KS[s][ROW_MAX:KROWS], ones.broadcast_to([3, H, S])).then_inc(ks_ld[s], 16)

            def zero_rows(rows, n):
                z = zeros_d.rearrange("a b -> (a b)").bitcast(BF16)[0:H * n]
                return z.rearrange("(o h n) -> o h n", o=1, h=H).broadcast_to([rows, H, n])

            def store_queries(g, i):
                sp.dma_start(q_parts[i, :, GC * g:GC * g + GC].rearrange("(k p) n -> p k n", p=P),
                             QP[:, i]).then_inc(q_st[g][i], 16)

            for i in (2, 3):
                sp.wait_ge(k_st[i], 16 * 3)
            sp.wait_ge(zero_st, 32)
            sp.wait_ge(ones_st, 16)
            sp.wait_ge(mask_st, 16)
            sp.wait_ge(aiv_mm, 3 * RT)
            load_keys(2)
            load_keys(3)
            sp.wait_ge(state, RT)
            load_keys(0)
            load_keys(1)
            sp.wait_ge(y_mm, 3 * B)
            sp.dma_start(QS[ROW_MASK:ROW_MASK + 1].rearrange("p h n -> p (h n)"),
                         ones_d.rearrange("a b -> (a b)")[0:H * N].unsqueeze(0)).then_inc(qs_one, 16)
            sp.dma_start(QS[ROW_MAX:P], zero_rows(P - ROW_MAX, N)).then_inc(qs_one, 16)
            for i in range(3):
                if i == 0:
                    sp.wait_ge(q4_out, 2)
                else:
                    sp.wait_ge(q4_split, i)
                store_queries(0, i)
            load_queries(sp, 0, 2)
            for b in range(B):
                sp.wait_ge(np_out, b + 1)
                for i in range(2):
                    load_maxima(sp, b, i)
                if b == 0:
                    for i in range(3):
                        sp.wait_ge(q4_split1, max(i, 1))
                        store_queries(1, i)
                    for i in range(3):
                        load_queries(sp, 1, i)
                if b >= 1 and b - 1 + KSLOTS < B:
                    sp.wait_ge(st_mm, HG * NJ * b)
                    load_keys(b - 1 + KSLOTS)
            for b in range(B):
                sp.wait_ge(x_new, B * (NBLOCKS - 1) + b + 1)
                sp.dma_start(out[b], X[:, b, :]).then_inc(out_st, 16)
            sp.wait_ge(out_st, 16 * B)
            sp.wait_ge(zero_st, 32)

        @block.gpsimd
        def _(pool):
            gp = nc.gpsimd
            link = Link(pool, pool_link)
            NQ = ALU.not_equal
            gp.memset(mhalf[:], -0.5)
            gp.memset(onesb[:], 1.0)
            link(gp.memset(identf[:], 0.0))
            link(gp.affine_select(out=identf[:], in_=identf[:], compare_op=NQ, fill=1.0, base=0,
                                  pattern=[[-1, P]], channel_multiplier=1))
            link(gp.memset(zrow[:], 0.0))
            gp.memset(onesf[:], 1.0).then_inc(consts, 1)
            link(gp.memset(M[:], 1.0))
            link(gp.affine_select(out=M[:], in_=M[:], compare_op=ALU.is_ge, fill=0.0, base=DK * 24,
                                  pattern=[[-DK, MW]], channel_multiplier=1))
            link(gp.affine_select(out=M[:], in_=M[:], compare_op=ALU.is_ge, fill=0.0,
                                  base=DK - 1 - DK * 24, pattern=[[DK, MW]], channel_multiplier=-1))
            gp.iota(negn[:], pattern=[[-1, B]], base=0, channel_multiplier=0,
                    allow_small_or_imprecise_dtypes=True).then_inc(consts, 1)
            def rsqrt(L):
                for g in range(G):
                    pool.wait_ge(var_ready, G * L + g + 1)
                    gp.tensor_tensor(rstd[:, GB * g:GB * g + GB], ve[:, GB * g:GB * g + GB], mhalf[:],
                                     ALU.pow).then_inc(rstd_ready, 1)

            rsqrt(0)
            pool.wait_ge(ld["pe"], 16)
            link(gp.tensor_tensor(DD[:], PE9[:, 1:NPOS], PE9[:, 0:B], ALU.subtract))
            gp.tensor_copy(CF[:, 0:1], PE9[:, 0:1])
            gp.tensor_copy(CF[:, 1:2], DD[:, 0:1])
            link(gp.tensor_tensor(CF[:, 2:NPOS], DD[:, 1:B], DD[:, 0:B - 1], ALU.subtract))
            gp.tensor_tensor(PEM[:], M[:].unsqueeze(1).broadcast_to([P, NPOS, MW]),
                             CF[:].unsqueeze(2).broadcast_to([P, NPOS, MW]), ALU.mult
                             ).then_inc(consts, 1)
            link(gp.memset(SELT[:], 0.0))
            sv = SELT[:].rearrange("p u (h d) -> p u h d", h=HH)
            gp.affine_select(out=sv, in_=sv, compare_op=NQ, fill=1.0, base=0,
                             pattern=[[-HH, B * KT], [-1, HH], [0, DK]], channel_multiplier=1
                             ).then_inc(consts, 1)

            def bias(L):
                if L in ROWBIAS:
                    pool.wait_ge(xn_ready, B * L + B)
                    pool.wait_ge(ld["rows"], 32)
                    gp.tensor_tensor(X[:], X[:], RB[:, ROWBIAS[L]].unsqueeze(1).broadcast_to([T, B, D]),
                                     ALU.add).then_inc(bias_added, 1)

            def split_key(b):
                i = k_buffer(b)
                if i == b % 2 and b >= 2:
                    pool.wait_ge(k_st[i], 16 * 3 * (b // 2))
                pool.wait_ge(side_out, SIDE.index(("k", b)) + 1)
                k32, parts = K32[i], KP[i]
                link(gp.tensor_tensor(k32, k32, parts[:, 0], ALU.subtract))
                link(gp.tensor_copy(parts[:, 1], k32))
                gp.tensor_tensor(parts[:, 2], k32, parts[:, 1], ALU.subtract).then_inc(k_split, 1)

            pool.wait_ge(qkv_out, 8)
            q0, k0 = QKV[1], QKV[0]
            for i, u in enumerate(POOL_UNITS):
                s, k = UNITS[u]
                if i >= 2:
                    pool.wait_ge(prod_used, POOL_UNITS[i - 2] + 1)
                gp.tensor_tensor(PB[PSLOT[u]], k0[:, k].rearrange("p (s t) -> p s t", s=B),
                                 q0[:, k, s * T:s * T + T].unsqueeze(1).broadcast_to([P, B, T]),
                                 ALU.mult).then_inc(prod_pool, 1)
            link(gp.memset(tri[:], 1.0))
            gp.affine_select(out=tri[:], in_=tri[:], compare_op=ALU.is_ge, fill=0.0, base=0,
                             pattern=[[1, T]], channel_multiplier=-1)
            link(gp.memset(selb[:], 0.0))
            link(gp.affine_select(out=selb[:], in_=selb[:], compare_op=NQ, fill=1.0, base=0,
                                  pattern=[[-1, B], [0, T]], channel_multiplier=1))
            gp.tensor_copy(identb[:], identf[:])
            gp.iota(ev8[:], pattern=[[0, B], [-1, E]], base=E, channel_multiplier=0,
                    allow_small_or_imprecise_dtypes=True).then_inc(consts, 1)
            link(gp.memset(PICK[:], 0.0))
            pv = PICK[:].rearrange("p (c w) -> p c w", c=HG)
            gp.affine_select(out=pv, in_=pv, compare_op=NQ, fill=1.0, base=0,
                             pattern=[[-32, HG], [-1, VW]], channel_multiplier=1
                             ).then_inc(consts, 1)
            pool.wait_ge(ld["masks"], 32)
            gp.tensor_scalar(mkx[:], mki[:], 0, MASKED, ALU.is_equal, ALU.mult).then_inc(masks_ready, 1)
            gp.tensor_scalar(mk4[:], mk8[:], 0, MASKED, ALU.is_equal, ALU.mult).then_inc(masks_ready, 1)
            for b in range(2):
                split_key(b)
            bias(0)
            for i, u in enumerate(SUM_POOL):
                s, k = u // KT, u % KT
                w = PB[SSLOT[u]].rearrange("p s t -> p (s t)")
                pool.wait_ge(spread_used, u + 1)
                for n in (4 * T, 2 * T):
                    link(gp.tensor_tensor(w[:, 0:n], w[:, 0:n], w[:, n:2 * n], ALU.add))
                gp.tensor_tensor(O0[:, k, s * T:s * T + T], w[:, 0:T], w[:, T:2 * T], ALU.add
                                 ).then_inc(sum_pool, 1)
            rsqrt(1)
            pool.wait_ge(spread_used, 2 * B)
            gp.memset(V4[:, :, :, DK:VW], 1.0).then_inc(v_ones, 1)
            split_key(2)
            bias(1)
            for b in range(3, 6):
                split_key(b)
            rsqrt(2)
            pool.wait_ge(slots_ready, 1)
            pool.wait_ge(zero_st, 32)
            for b in range(B):
                pool.wait_ge(xg_ready, b + 1)
                gp.indirect_dma_start(
                    slots_in, bass.IndirectOffsetOnAxis(ap=tb(11).bitcast(U32)[:, b:b + 1], axis=0),
                    XN[:, b, :], None, bounds_check=N - 1, oob_is_err=False).then_inc(scat, 16)
            split_key(6)
            split_key(7)
            pool.wait_ge(eo_st, 16 * E // 2)
            pool.wait_ge(xst_ready, 4)
            for b in range(B):
                gp.indirect_dma_start(
                    XN[:, b, :], None, slots_out,
                    bass.IndirectOffsetOnAxis(ap=tb(12).bitcast(U32)[:, b:b + 1], axis=0)
                ).then_inc(gat[b], 16)
            rsqrt(3)
            pool.wait_ge(side_mm, len(SIDE))
            for i in (2, 3):
                pool.wait_ge(k_st[i], 16 * 3)
            gp.memset(DEC[:, :, :, 0:1], 0.0)
            gp.memset(UU[:, :, :, 0:1], 0.0)
            for t in BT:
                link(gp.memset(t, 0.0))
            gp.memset(BT[0][:, :, 0:1], 1.0 / FLOOR)
            gp.memset(BT[1][:, :, 0:1], 1.0 / FLOOR).then_inc(pads, 1)
            bias(3)
            for j in range(RT):
                pool.wait_ge(clamped, j + 1)
                if j >= 4:
                    pool.wait_ge(u_done, j - 3)
                gp.tensor_tensor(SQ[j % 4], DEC[:, j], DEC[:, j], ALU.mult).then_inc(squares, 1)
            rsqrt(4)
            bias(4)
            pool.wait_ge(q4_out, 4)
            link(gp.tensor_tensor(QW, QW, QP[:, 0], ALU.subtract))
            gp.tensor_copy(QP[:, 1], QW).then_inc(q4_split1, 1)
            pool.wait_ge(q4_split1, 1)
            gp.tensor_tensor(QP[:, 2], QW, QP[:, 1], ALU.subtract).then_inc(q4_split1, 1)
            for b in range(B):
                i = b % 2
                pool.wait_ge(mx_out, PAIRS * (b + 1))
                if b >= 2:
                    pool.wait_ge(np_tr, b - 1)
                link(gp.tensor_copy(NP[:, i, 0], NM[:, i]))
                link(gp.tensor_tensor(NM[:, i], NM[:, i], NP[:, i, 0], ALU.subtract))
                link(gp.tensor_copy(NP[:, i, 1], NM[:, i]))
                gp.tensor_tensor(NP[:, i, 2], NM[:, i], NP[:, i, 1], ALU.subtract).then_inc(np_ready, 1)
                pool.wait_ge(np_out, b + 1)
                load_maxima(pool, b, 2)
            rsqrt(5)

        @block.scalar
        def _(act):
            sc = nc.scalar
            link = Link(act, act_link)
            done = [0]

            def xt_out(tr, first, ready, groups=range(G)):
                for g in groups:
                    act.wait_ge(tr, first + g + 1)
                    sc.activation(XT[:, :, GC * g:GC * g + GC], PP[g][:, :, 0:GC], ACT.Copy
                                  ).then_inc(ready, KT)

            def side(point):
                for i in side_items(point, done):
                    kind, b = SIDE[i]
                    lo, hi = PS[side_bank(i)], PS[side_bank(i) + 1]
                    act.wait_ge(side_mm, i + 1)
                    if kind == "qk":
                        act.wait_ge(ld["cb"], 16)
                        sc.activation(WQK[:].rearrange("p k d -> p (k d)"), lo, ACT.Copy)
                        sc.activation(BQ16[:], hi[:, 0:KT], ACT.Copy, scale=1 / 16)
                        sc.activation(BQ4[:], CB[:, C_BQ1:C_BQ1 + KT], ACT.Copy, scale=1 / 4
                                      ).then_inc(side_out, 1)
                    elif kind == "k":
                        buf = k_buffer(b)
                        if buf == b % 2 and b >= 2:
                            act.wait_ge(k_split, b - 1)
                            act.wait_ge(k_st[buf], 16 * 3 * (b // 2))
                        for k in range(KT):
                            c = CB[:, C_BK1 + k:C_BK1 + k + 1]
                            sc.activation(K32[buf][:, k], (lo, hi)[k][:, 0:S], ACT.Identity, bias=c)
                            ins = sc.activation(KP[buf][:, 0, k], (lo, hi)[k][:, 0:S], ACT.Identity, bias=c)
                        ins.then_inc(side_out, 1)
                    elif kind == "f":
                        sc.activation(fs[:, 1:2], hi[:, 0:1], ACT.Copy).then_inc(side_out, 1)
                    else:
                        act.wait_ge(v_ones, 1)
                        d = V4[:, NJ * b:NJ * b + NJ, :, 0:DK]
                        n0, n2 = SJ[0][1], SJ[2][1]
                        sc.activation(d[0:n0, 0:2], lo[0:n0, :].rearrange("p (j h d) -> p j h d", j=2, h=H),
                                      ACT.Copy)
                        sc.activation(d[0:n2, 2], hi[0:n2, 0:D].rearrange("p (h d) -> p h d", h=H),
                                      ACT.Copy).then_inc(side_out, 1)

            xt_out(xn_tr, 0, xt_ready)
            act.wait_ge(ld["cb"], 16)
            for i in range(12):
                w, g, m = i // 4, i // 2 % 2, i % 2
                c = (C_BK0, C_BQ0, C_BV0)[w] + m
                act.wait_ge(qkv_mm, i + 1)
                sc.activation(QKV[w][:, m, GC * g:GC * g + GC], PS[4 + i % 2][:, 0:GC], ACT.Identity,
                              bias=CB[:, c:c + 1]).then_inc(qkv_out, 1)
            act.wait_ge(prod_used, len(UNITS))
            for g in range(G):
                ins = sc.activation(GA[:, GB * g:GB * g + GB], PS[g][:, 0:GC].rearrange("p (s t) -> p s t", s=GB),
                                    ACT.Sigmoid, scale=0.25)
            ins.then_inc(gates, 1)
            act.wait_ge(consts, 2)
            act.wait_ge(pos_ready, 1)
            at = 0
            for n in range(1, B):
                sc.activation(R0[:, at:at + (B - n) * T], GA[:, 0:B - n].rearrange("p s t -> p (s t)"),
                              ACT.Relu, bias=negn[:, n:n + 1]).then_inc(relus, 1)
                at += (B - n) * T
            side("cope")
            act.wait_ge(shifted, 1)
            sc.activation(AL, AL, ACT.Exp).then_inc(exp0, 1)
            xt_out(xn_tr, G, xt_ready, [0])
            side("ln1")
            xt_out(xn_tr, G, xt_ready, [1])
            for i in range(4):
                g, m = i // 2, i % 2
                act.wait_ge(qk_mm, i + 1)
                sc.activation(QK[:, m, GC * g:GC * g + GC], PS[4 + m][:, 0:GC], ACT.Identity,
                              bias=BQ16[:, m:m + 1], scale=1 / 16).then_inc(qk_out, 1)
            for i in range(B + 1):
                if i < B:
                    act.wait_ge(sc_max, i + 1)
                    if i >= 2:
                        act.wait_ge(pt_mm, i - 1)
                    sc.activation(PX[i % 2][0:T], PS[i % 2][0:T, 0:S], ACT.Exp, bias=tb(0)[:, i:i + 1],
                                  accum_out=tb(1)[:, i:i + 1]).then_inc(sc_exp, 1)
                if i >= 1:
                    b = i - 1
                    act.wait_ge(pt_mm, b + 1)
                    if b >= 2:
                        act.wait_ge(pc_mm, b - 1)
                    n0, n2 = SJ[0][1], SJ[2][1]
                    bank = PS[2][:, 0:NJ * T].rearrange("p (j t) -> p j t", j=NJ)
                    sc.activation(PT1[b % 2][0:n0, 0:2], bank[0:n0, 0:2], ACT.Copy).then_inc(pt_out, 1)
                    sc.activation(PT1[b % 2][0:n2, 2], bank[0:n2, 2], ACT.Copy).then_inc(pt_out, 1)
                side(f"b1_{i}")
            xt_out(xn_tr, 2 * G, xt_ready, [0])
            side("ln2")
            xt_out(xn_tr, 2 * G, xt_ready, [1])
            act.wait_ge(rt_shift, 1)
            sc.activation(tiny(3), tiny(2), ACT.Exp).then_inc(rt_exp, 1)
            side("router")
            side("route")
            xt_out(xs_tr, 0, xst_ready)
            for e in range(E):
                act.wait_ge(h_mm, e + 1)
                if e >= 2:
                    act.wait_ge(eo_mm, e - 1)
                for m in range(KT):
                    c = C_B1 + KT * e + m
                    ins = sc.activation(HT[e % 2][:, m], PS[4 + e % 2][:, m * CAP:(m + 1) * CAP], ACT.Relu,
                                        bias=CB[:, c:c + 1])
                ins.then_inc(h_out, 1)
            side("gather")
            xt_out(xn_tr, 3 * G, xt_ready)
            act.wait_ge(pads, 1)
            for j in range(RT):
                for w, dst in ((0, DEC), (1, UU)):
                    i = 3 * j + w
                    act.wait_ge(aiv_mm, i + 1)
                    for g in range(G):
                        src = PS[2 * aiv_pair(i) + g][:, 0:GC].rearrange("p (b t) -> p b t", b=GB)
                        o = dst[:, j, GB * g:GB * g + GB, 1:TP]
                        if w == 0:
                            ins = sc.activation(o, src, ACT.Sigmoid, bias=CB[:, C_DEC + j:C_DEC + j + 1])
                        else:
                            ins = sc.activation(o, src, ACT.Sigmoid)
                    ins.then_inc(sig, 1)
                if j % 4 == 3:
                    for jj in range(j - 3, j + 1):
                        act.wait_ge(squares, jj + 1)
                        sc.activation(SQ[jj % 4], SQ[jj % 4], ACT.Sqrt, scale=-1.0, bias=onesf[:, 0:1]
                                      ).then_inc(roots, 1)
            for i in range(4):
                g, m = i // 2, i % 2
                if m == 0:
                    xt_out(xn_tr, 4 * G, xt_ready, [g])
                act.wait_ge(q4_mm, i + 1)
                if i == 2:
                    load_queries(act, 0, 0)
                    load_queries(act, 0, 1)
                    act.wait_ge(q4_split, 2)
                    act.wait_ge(q_st[0][2], 16)
                sc.activation(QW[:, m], PS[4 + m][:, 0:GC], ACT.Identity, bias=BQ4[:, m:m + 1], scale=1 / 4)
                sc.activation(QP[:, 0, m], PS[4 + m][:, 0:GC], ACT.Identity, bias=BQ4[:, m:m + 1],
                              scale=1 / 4).then_inc(q4_out, 1)

            def exps(b, u):
                w = UNITS4 * b + u
                j, g = u // HG, u % HG
                slot = (NJ * b + j) % PSLOTS
                act.wait_ge(st_mm, w + 1)
                if NJ * b + j >= PSLOTS and g == 0:
                    act.wait_ge(pv_mm, HG * (NJ * b + j - PSLOTS + 1))
                n = SJ[j][1]
                sc.activation(P4[slot][0:n, g * HG * T:(g + 1) * HG * T], PS[4 + w % 2][0:n, 0:HG * T],
                              ACT.Exp).then_inc(st_exp, 1)

            def parts_out(b, _):
                act.wait_ge(np_tr, b + 1)
                if b >= 2:
                    act.wait_ge(nm_ld[0][b % 2], 16 * 2 * (b // 2))
                    act.wait_ge(nm_ld[1][b % 2], 16 * (b // 2))
                sc.activation(NT[b % 2][:], NPT, ACT.Copy).then_inc(np_out, 1)

            def os_evac(b, _):
                act.wait_ge(pv_mm, UNITS4 * (b + 1))
                if b >= 1:
                    act.wait_ge(os_tr, b)
                sc.activation(OS, PS[6][:, 0:HG * T], ACT.Copy).then_inc(os_out, 1)

            def ot_evac(b, _):
                act.wait_ge(on_tr, b + 1)
                if b >= 2:
                    act.wait_ge(y_mm, y_before(4) + b - 1)
                for k in range(KT):
                    c = C_BV1 + k
                    ins = sc.activation(OT[b % 2][:, k], ONT[:, k], ACT.Identity, bias=CB[:, c:c + 1])
                ins.then_inc(ot_out, 1)

            run_block4(scores=exps, parts=parts_out, os_evac=os_evac, out_tr=ot_evac)
            xt_out(xn_tr, 5 * G, xt_ready)

        @block.tensor
        def _(pe):
            mm = nc.tensor.matmul
            done = [0]

            def transposes(first, g, tr=xn_tr):
                for j in range(GB):
                    b = GB * g + j
                    if first is not None:
                        pe.wait_ge(xn_ready, first + b + 1)
                    for k in range(KT):
                        ins = nc.tensor.transpose(PS[2 * g + k][:, j * T:j * T + T],
                                                  XN[:, b, k * P:(k + 1) * P], identf[0:T, 0:T])
                ins.then_inc(tr, 1)

            def project(r, lhs, rhs, bank):
                if bank is None:
                    bank = PS[4 + r % 2]
                    if r >= 2:
                        pe.wait_ge(x_new, r - 1)
                for k in range(KT):
                    ins = mm(bank[0:T, 0:D], lhs(k), rhs(k), start=(k == 0), stop=(k == KT - 1))
                ins.then_inc(y_mm, 1)

            def side(point):
                for i in side_items(point, done):
                    kind, b = SIDE[i]
                    lo, hi = PS[side_bank(i)], PS[side_bank(i) + 1]
                    if side_before(i):
                        pe.wait_ge(side_out, side_before(i))
                    if kind == "qk":
                        pe.wait_ge(ld["wx"], 48)
                        pe.wait_ge(ld["cb"], 16)
                        for m in range(KT):
                            for k in range(KT):
                                mm(lo[:, m * D:(m + 1) * D], WX[:, 0, k, m * P:(m + 1) * P], WX[:, 1, k, :],
                                   start=(k == 0), stop=(k == KT - 1))
                        for m in range(KT):
                            for k in range(KT):
                                ins = mm(hi[:, m:m + 1], WX[:, 1, k, m * P:(m + 1) * P],
                                         CB[:, C_BQX + k:C_BQX + k + 1], start=(k == 0), stop=(k == KT - 1))
                    elif kind == "k":
                        pe.wait_ge(ld["w4"], 64)
                        pe.wait_ge(ld["ct"], 32)
                        if b == 2:
                            pe.wait_ge(x_new, B)
                        for m in range(KT):
                            for k in range(KT):
                                ins = mm((lo, hi)[m][:, 0:S], W4[:, 0, k, m * P:(m + 1) * P],
                                         CT[:, k, b * S:(b + 1) * S], start=(k == 0), stop=(k == KT - 1))
                    elif kind == "f":
                        pe.wait_ge(asum, 1)
                        ins = mm(hi[:, 0:1], onesf[:], fs[:, 3:4], start=True, stop=True)
                    else:
                        if b == 0:
                            pe.wait_ge(v_ones, 1)
                        for j, (s0, n) in enumerate(SJ):
                            o = lo[0:n, j * D:(j + 1) * D] if j < 2 else hi[0:n, 0:D]
                            for k in range(KT):
                                ins = mm(o, CT[:, k, b * S + s0:b * S + s0 + n], W4[:, 1, k, :],
                                         start=(k == 0), stop=(k == KT - 1))
                    ins.then_inc(side_mm, 1)

            pe.wait_ge(consts, 1)
            transposes(0, 0)
            transposes(0, 1)
            pe.wait_ge(ld["w0"], 64)
            for i in range(12):
                w, g, m = i // 4, i // 2 % 2, i % 2
                pe.wait_ge(xt_ready, KT * (g + 1))
                if i >= 2:
                    pe.wait_ge(qkv_out, i - 1)
                for k in range(KT):
                    ins = mm(PS[4 + i % 2][:, 0:GC], W0[:, w, k, m * P:(m + 1) * P], XT[:, k, GC * g:GC * g + GC],
                             start=(k == 0), stop=(k == KT - 1))
                ins.then_inc(qkv_mm, 1)
            pe.wait_ge(consts, 3)
            pe.wait_ge(qkv_out, 8)
            pe.wait_ge(xt_ready, KT * G)
            def cope(n):
                bank, c0 = (PS[2], n * T) if n < 5 else (PS[3], (n - 5) * T)
                for odd in range(2):
                    for k in range(KT):
                        x0 = 24 - (16 * odd + HH * k)
                        for c in range(4):
                            s = 2 * c + odd
                            ins = mm(bank[32 * c:32 * c + 32, c0:c0 + T], PEM[:, n, x0:x0 + 32],
                                     QKV[1][:, k, s * T:s * T + T], start=(odd == 0 and k == 0),
                                     stop=(odd == 1 and k == 1))
                ins.then_inc(cope_mm, 1)

            nd = npl = 0
            for u, (s, k) in enumerate(UNITS):
                odd, c = s % 2, s // 2
                if u in POOL_UNITS:
                    npl += 1
                    pe.wait_ge(prod_pool, npl)
                else:
                    nd += 1
                    pe.wait_ge(prod_dve, nd)
                x0 = 24 - (16 * odd + HH * k)
                for g in range(G):
                    ins = mm(PS[g][32 * c:32 * c + 32, 0:GC], M[:, x0:x0 + 32],
                             PB[PSLOT[u]][:, GB * g:GB * g + GB].rearrange("p s t -> p (s t)"),
                             start=(odd == 0 and k == 0), stop=(odd == 1 and k == 1))
                ins.then_inc(prod_used, 1)
                if u % 2 == 0:
                    cope(u // 2)
            cope(NPOS - 1)
            pe.wait_ge(qkv_out, 12)
            side("cope")

            def project0(b):
                units = range(KT * b + KT)
                pe.wait_ge(sum_dve, sum(u in SUM_DVE for u in units))
                if any(u in SUM_POOL for u in units):
                    pe.wait_ge(sum_pool, sum(u in SUM_POOL for u in units))
                if b >= 2:
                    pe.wait_ge(x_new, b - 1)
                project(b, lambda k: O0[:, k, b * T:b * T + T], lambda k: W0[:, 3, k, :], PS[6 + b % 2])

            pe.wait_ge(probs0, 1)
            pe.wait_ge(consts, 4)
            pe.wait_ge(qkv_out, 12)
            pe.wait_ge(side_out, SIDE_AT["cope"])
            for u in range(KT * B):
                if u >= 3:
                    pe.wait_ge(spread_used, u - 2)
                for g in range(G):
                    ins = mm(PS[2 * (u % 3) + g][:, 0:GC], SELT[:, u],
                             AL[:, GB * g:GB * g + GB].rearrange("p s t -> p (s t)"), start=True, stop=True)
                ins.then_inc(spread_mm, 1)
                if u >= 5 and u % 2:
                    project0((u - 5) // 2)
            project0(B - 2)
            project0(B - 1)
            pe.wait_ge(spread_used, KT * B)
            transposes(B, 0)
            side("ln1")
            transposes(B, 1)
            for i in range(4):
                g, m = i // 2, i % 2
                pe.wait_ge(xt_ready, KT * G + KT * (g + 1))
                if i >= 2:
                    pe.wait_ge(qk_out, i - 1)
                for k in range(KT):
                    ins = mm(PS[4 + m][:, 0:GC], WQK[:, k, m * P:(m + 1) * P], XT[:, k, GC * g:GC * g + GC],
                             start=(k == 0), stop=(k == KT - 1))
                ins.then_inc(qk_mm, 1)
            pe.wait_ge(ld["cn"], 16 * NJ)
            pe.wait_ge(masks_ready, 1)
            pe.wait_ge(consts, 5)
            pe.wait_ge(qk_out, 4)
            for i in range(B + 3):
                if i < B:
                    b = i
                    if b >= 2:
                        pe.wait_ge(sc_exp, b - 1)
                    o = PS[b % 2][0:T, 0:S]
                    for k in range(KT):
                        mm(o, QK[:, k, b * T:b * T + T], CT[:, k, b * S:(b + 1) * S], start=(k == 0), stop=False)
                    mm(o, selb[:, b, :], mkx[:], start=False, stop=True).then_inc(sc_mm, 1)
                if 1 <= i <= B:
                    b = i - 1
                    pe.wait_ge(sc_exp, b + 1)
                    if b >= 1:
                        pe.wait_ge(pt_out, 2 * b)
                    for j, (s0, n) in enumerate(SJ):
                        ins = nc.tensor.transpose(PS[2][0:n, j * T:j * T + T], PX[b % 2][0:T, s0:s0 + n],
                                                  identf[0:T, 0:T])
                    ins.then_inc(pt_mm, 1)
                if 2 <= i <= B + 1:
                    b = i - 2
                    pe.wait_ge(pt_out, 2 * (b + 1))
                    if b >= 1:
                        pe.wait_ge(pc_out, b)
                    for m in range(KT):
                        for j, (s0, n) in enumerate(SJ):
                            ins = mm(PS[3][:, m * T:m * T + T], CN[0:n, j, b, m * P:(m + 1) * P],
                                     PT1[b % 2][0:n, j], start=(j == 0), stop=(j == NJ - 1))
                    ins.then_inc(pc_mm, 1)
                if i >= 3:
                    b = i - 3
                    pe.wait_ge(pc_out, b + 1)
                    project(B + b, lambda k: PC[:, k, b * T:b * T + T], lambda k: WX[:, 2, k, :], None)
                side(f"b1_{i}")
            transposes(2 * B, 0)
            side("ln2")
            transposes(2 * B, 1)
            pe.wait_ge(x_new, 2 * B)
            pe.wait_ge(ld["wr"], 16)
            for b in range(B):
                pe.wait_ge(xt_ready, 2 * KT * G + KT * (b // GB + 1))
                for k in range(KT):
                    ins = mm(PS[4][0:T, b * E:(b + 1) * E], XT[:, k, b * T:b * T + T], WR[:, k, :],
                             start=(k == 0), stop=(k == KT - 1))
            ins.then_inc(rt_mm, 1)
            side("router")
            pe.wait_ge(onehot, 1)
            oh = tiny(9).bitcast(BF16)
            mm(PS[5][0:T, 0:B * E], tri[:], oh[:, 0:B * E], start=True, stop=False)
            mm(PS[5][0:T, 0:B * E], onesb[0:T, 0:T], oh[:, B * E:2 * B * E], start=False, stop=True
               ).then_inc(pos_mm, 1)
            side("route")
            for g in range(G):
                pe.wait_ge(xs_ld[g], 16)
                transposes(None, g, xs_tr)
            pe.wait_ge(xst_ready, KT * G)
            pe.wait_ge(ld["w1"], 16)
            pe.wait_ge(ld["w2"], 16)
            pe.wait_ge(xg_ready, B)
            pe.wait_ge(side_out, SIDE_AT["route"])
            for i in range(E + 1):
                if i < E:
                    e = i
                    if e >= 2:
                        pe.wait_ge(h_out, e - 1)
                    for m in range(KT):
                        for k in range(KT):
                            ins = mm(PS[4 + e % 2][:, m * CAP:(m + 1) * CAP], W1[:, e, k, m * P:(m + 1) * P],
                                     XT[:, k, e * CAP:(e + 1) * CAP], start=(k == 0), stop=(k == KT - 1))
                    ins.then_inc(h_mm, 1)
                if i >= 1:
                    e = i - 1
                    pe.wait_ge(h_out, e + 1)
                    if e >= 2:
                        pe.wait_ge(eo_out, e - 1)
                    for k in range(KT):
                        ins = mm(PS[6 + e % 2][0:CAP, 0:D], HT[e % 2][:, k], W2[:, e, k, :],
                                 start=(k == 0), stop=(k == KT - 1))
                    ins.then_inc(eo_mm, 1)
            pe.wait_ge(eo_out, E)
            side("gather")
            def aiv(i, g):
                j, w = i // 3, i % 3
                for k in range(KT):
                    c = w * REC + j * P
                    ins = mm(PS[2 * aiv_pair(i) + g][:, 0:GC], WA[:, k, c:c + P], XT[:, k, GC * g:GC * g + GC],
                             start=(k == 0), stop=(k == KT - 1))
                return ins

            transposes(3 * B, 0)
            pe.wait_ge(side_out, len(SIDE))
            pe.wait_ge(ld["wa"], 16)
            pe.wait_ge(xt_ready, 3 * KT * G + KT)
            for i in range(2):
                aiv(i, 0)
            transposes(3 * B, 1)
            pe.wait_ge(xt_ready, 4 * KT * G)
            for i in range(3 * RT):
                if i >= 4:
                    jp, wp = (i - 4) // 3, (i - 4) % 3
                    if wp < 2:
                        pe.wait_ge(sig, 2 * jp + wp + 1)
                    else:
                        pe.wait_ge(iv_done, jp + 1)
                if i >= 2:
                    aiv(i, 0)
                aiv(i, 1).then_inc(aiv_mm, 1)
            pe.wait_ge(iv_done, RT)
            pe.wait_ge(sig, 2 * RT)
            pe.wait_ge(ld["wmix"], 16)
            for j in range(RT // 2):
                pe.wait_ge(state, j + 1)
                for b in range(B):
                    mm(PS[b][0:T, 0:D], UU[:, j, b, 1:TP], WMIX[:, j, :], start=(j == 0), stop=False)
            for b in range(B):
                for j in range(RT // 2, RT):
                    pe.wait_ge(state, j + 1)
                    ins = mm(PS[b][0:T, 0:D], UU[:, j, b, 1:TP], WMIX[:, j, :], start=False,
                             stop=(j == RT - 1))
                ins.then_inc(y_mm, 1)
            pe.wait_ge(x_new, 3 * B + 6)
            for i in range(4):
                g, m = i // 2, i % 2
                if m == 0:
                    transposes(4 * B, g)
                pe.wait_ge(xt_ready, 4 * KT * G + KT * (g + 1))
                if i >= 2:
                    pe.wait_ge(q4_out, i - 1)
                for k in range(KT):
                    ins = mm(PS[4 + m][:, 0:GC], W4[:, 2, k, m * P:(m + 1) * P], XT[:, k, GC * g:GC * g + GC],
                             start=(k == 0), stop=(k == KT - 1))
                ins.then_inc(q4_mm, 1)
            pe.wait_ge(x_new, 4 * B)
            pe.wait_ge(pv_zero, 1)
            pe.wait_ge(consts, 6)
            pe.wait_ge(qs_one, 32)
            pe.wait_ge(ks_zero, 16 * KSLOTS)
            pe.wait_ge(xt_ready, 5 * KT * G)

            def maxima(b, i):
                if i == 0:
                    pe.wait_ge(ks_ld[b % KSLOTS], 16 * 8 * (b // KSLOTS + 1))
                    pe.wait_ge(qs_ld[b // GB], 16 * 6)
                w = PAIRS * b + i
                if w >= 2:
                    pe.wait_ge(mx_out, w - 1)
                for c in range(2):
                    h = 2 * i + c
                    ins = mm(PP[w % 2][0:T, c, 0:S], QS[:, h, b * T:b * T + T],
                             KS[b % KSLOTS][:, h, :], start=True, stop=True)
                ins.then_inc(mx_mm, 1)

            def parts_tr(b, _):
                pe.wait_ge(np_ready, b + 1)
                if b >= 1:
                    pe.wait_ge(np_out, b)
                if b >= 2:
                    pe.wait_ge(on_ready, b - 1)
                nc.tensor.transpose(NPT, NP[:, b % 2].rearrange("p i h -> p (i h)"), identb[0:T, 0:T]
                                    ).then_inc(np_tr, 1)

            def scores(b, u):
                j, g = u // HG, u % HG
                s0, n = SJ[j]
                w = UNITS4 * b + u
                if u == 0:
                    pe.wait_ge(nm_ld[0][b % 2], 16 * 2 * (b // 2 + 1))
                    pe.wait_ge(nm_ld[1][b % 2], 16 * (b // 2 + 1))
                if w == 0:
                    pe.wait_ge(q4_out, 4)
                if w >= 2:
                    pe.wait_ge(st_exp, w - 1)
                for c in range(HG):
                    h = HG * g + c
                    ins = mm(PS[4 + w % 2][0:n, c * T:c * T + T], KS[b % KSLOTS][:, h, s0:s0 + n],
                             QS[:, h, b * T:b * T + T], start=True, stop=True)
                ins.then_inc(st_mm, 1)

            def weighted(b, u):
                j, g = u // HG, u % HG
                n = SJ[j][1]
                if u == 0 and b >= 1:
                    pe.wait_ge(os_out, b)
                pe.wait_ge(st_exp, UNITS4 * b + u + 1)
                for c in range(4):
                    h = HG * g + c
                    ins = mm(PS[6][32 * c:32 * c + VW, g * T:g * T + T], V4[0:n, NJ * b + j, h, :],
                             P4[(NJ * b + j) % PSLOTS][0:n, h * T:h * T + T],
                             start=(u == 0), stop=(j == NJ - 1), skip_group_check=True)
                ins.then_inc(pv_mm, 1)

            def sums_tr(b, _):
                pe.wait_ge(os_out, b + 1)
                pe.wait_ge(np_out, min(B, b + 2))
                if b >= 1:
                    pe.wait_ge(x_new, 4 * B + b)
                for g in range(HG):
                    ins = mm(PS[7][0:T, g * HG * VW:(g + 1) * HG * VW], OS[:, g * T:g * T + T], PICK[:],
                             start=True, stop=True)
                ins.then_inc(os_tr, 1)

            def out_tr(b, _):
                pe.wait_ge(on_ready, b + 1)
                pe.wait_ge(np_out, min(B, b + 3))
                for k in range(KT):
                    ins = nc.tensor.transpose(ONT[:, k], zrow[:][:, k * P:(k + 1) * P], identf[0:T, 0:T])
                ins.then_inc(on_tr, 1)

            def out_mm(b, _):
                pe.wait_ge(ot_out, b + 1)
                project(4 * B + b, lambda k: OT[b % 2][:, k], lambda k: W4[:, 3, k, :], Y4)

            run_block4(maxima=maxima, parts=parts_tr, scores=scores, weighted=weighted,
                       sums_tr=sums_tr, out_tr=out_tr, out_mm=out_mm)
            pe.wait_ge(wf_ready, 1)
            for b in range(B):
                if b % GB == 0:
                    transposes(5 * B, b // GB)
                    pe.wait_ge(xt_ready, 5 * KT * G + KT * (b // GB + 1))
                if b >= 3:
                    pe.wait_ge(x_new, 5 * B + b - 3)
                project(5 * B + b, lambda k: XT[:, k, b * T:b * T + T], lambda k: WN[:, k, :], PS[4 + b % 4])

        @block.vector
        def _(dve):
            v = nc.vector
            link = Link(dve, dve_link)

            def stats(L, b):
                if L == 0:
                    dve.wait_ge(ld_x[b // GB], 16)
                else:
                    dve.wait_ge(x_new, B * (L - 1) + b + 1)
                v.bn_stats(st6[:, b], X[:, b]).then_inc(stats_done, 1)

            def aggregate(L, b):
                dve.wait_ge(stats_done, B * L + b + 1)
                v.bn_aggr(mv[:, b], st6[:, b]).then_inc(aggregated, 1)

            def variance(L, g):
                sl = slice(GB * g, GB * g + GB)
                dve.wait_ge(aggregated, B * L + GB * (g + 1))
                v.tensor_scalar(ve[:, sl], mv[:, sl, 1], EPS, None, ALU.add).then_inc(var_ready, 1)

            def norm(L, g):
                dve.wait_ge(rstd_ready, G * L + g + 1)
                for b in range(GB * g, GB * g + GB):
                    v.tensor_scalar(XN[:, b], X[:, b], mv[:, b, 0:1], rstd[:, b:b + 1], ALU.subtract, ALU.mult
                                    ).then_inc(xn_ready, 1)

            def after(L, b):
                if L + 1 >= NBLOCKS:
                    return
                if b >= 1:
                    stats(L + 1, b - 1)
                if b >= 2:
                    aggregate(L + 1, b - 2)
                if b == GB + 1:
                    variance(L + 1, 0)
                if b == B - 2:
                    norm(L + 1, 0)
                if b == B - 1:
                    stats(L + 1, b)
                    aggregate(L + 1, b - 1)
                    aggregate(L + 1, b)
                    variance(L + 1, 1)
                    norm(L + 1, 1)

            def add(L, b, bank):
                dve.wait_ge(y_mm, y_before(L) + b + 1)
                if b == 0:
                    dve.wait_ge(bias_added, sum(l in ROWBIAS for l in range(L + 1)))
                v.tensor_tensor(X[:, b], X[:, b], bank[0:T, 0:D], ALU.add).then_inc(x_new, 1)
                after(L, b)

            for g in range(G):
                for b in range(GB * g, GB * g + GB):
                    stats(0, b)
                for b in range(GB * g, GB * g + GB):
                    aggregate(0, b)
                variance(0, g)
            norm(0, 0)
            norm(0, 1)
            dve.wait_ge(qkv_out, 8)
            dve.wait_ge(consts, 1)
            q0, k0, v0 = QKV[1], QKV[0], QKV[2]
            for i, u in enumerate(DVE_UNITS):
                s, k = UNITS[u]
                if i >= 3:
                    dve.wait_ge(prod_used, DVE_UNITS[i - 3] + 1)
                v.tensor_tensor(PB[PSLOT[u]], k0[:, k].rearrange("p (s t) -> p s t", s=B),
                                q0[:, k, s * T:s * T + T].unsqueeze(1).broadcast_to([P, B, T]),
                                ALU.mult).then_inc(prod_dve, 1)
            dve.wait_ge(ld["wf"], 16)
            v.tensor_reduce(fs[:, 3:4], WF[:], AX.XY, ALU.add, apply_absolute_value=True).then_inc(asum, 1)
            dve.wait_ge(gates, 1)
            for s in range(B - 2, -1, -1):
                ins = v.tensor_tensor(GA[:, s], GA[:, s], GA[:, s + 1], ALU.add)
                if s:
                    link(ins)
            ins.then_inc(pos_ready, 1)
            dve.wait_ge(pos_ready, 1)
            dve.wait_ge(cope_mm, NPOS)

            def coef(n, keys):
                bank, c0 = (PS[2], n * T) if n < 5 else (PS[3], (n - 5) * T)
                return bank[:, c0:c0 + T].unsqueeze(1).broadcast_to([P, keys, T])

            link(v.tensor_tensor(AC, GA, coef(1, B), ALU.mult))
            ins = v.tensor_tensor(AC, AC, coef(0, B), ALU.add)
            at, ramps = 0, []
            for n in range(1, B):
                r = R0[:, at:at + (B - n) * T].rearrange("p (s t) -> p s t", t=T)
                at += (B - n) * T
                ramps.append((n, r))
                dve.wait_ge(relus, n)
                ins = v.tensor_tensor(r, r, coef(n + 1, B - n), ALU.mult)
            link(ins)
            for n, r in ramps:
                link(v.tensor_tensor(AC[:, 0:B - n], AC[:, 0:B - n], r, ALU.add))
            dve.wait_ge(prod_used, len(UNITS))
            for g in range(G):
                ins = v.scalar_tensor_tensor(
                    out=AL[:, GB * g:GB * g + GB].rearrange("p s t -> p (s t)"), in0=PS[g][:, 0:GC], scalar=0.25,
                    in1=AC[:, GB * g:GB * g + GB].rearrange("p s t -> p (s t)"), op0=ALU.mult, op1=ALU.add)
            link(ins)
            by_token = AL.rearrange("p s t -> p t s")
            link(v.tensor_reduce(MX, by_token, AX.X, ALU.max))
            v.tensor_tensor(AL, AL, MX.unsqueeze(1).broadcast_to([P, B, T]), ALU.subtract).then_inc(shifted, 1)
            dve.wait_ge(exp0, 1)
            link(v.tensor_reduce(MX, by_token, AX.X, ALU.add))
            link(v.reciprocal(RS, MX))
            v.tensor_tensor(AL, AL, RS.unsqueeze(1).broadcast_to([P, B, T]), ALU.mult).then_inc(probs0, 1)
            dve.wait_ge(qkv_out, 12)
            nsp = 0
            for u in range(KT * B):
                s, k = u // KT, u % KT
                w = PB[SSLOT[u]]
                dve.wait_ge(spread_mm, u + 1)
                if u in SUM_POOL:
                    i = SUM_POOL.index(u)
                    if i >= 2:
                        dve.wait_ge(sum_pool, i - 1)
                elif SUM_DVE.index(u) >= 3:
                    dve.wait_ge(sum_dve, SUM_DVE.index(u) - 2)
                v.tensor_tensor(w.rearrange("p (g s) t -> p g (s t)", g=G), PP[u % 3][:, :, 0:GC],
                                v0[:, k].rearrange("p (g n) -> p g n", g=G), ALU.mult).then_inc(spread_used, 1)
                if u - 1 in SUM_DVE and u >= 1:
                    sum_keys(dve, v, u - 1, spread_used, sum_dve)
                if u >= 6 and u % 2 == 0:
                    add(0, (u - 6) // 2, PS[6 + (u - 6) // 2 % 2])
            if KT * B - 1 in SUM_DVE:
                sum_keys(dve, v, KT * B - 1, spread_used, sum_dve)
            for b in range(B - 3, B):
                add(0, b, PS[6 + b % 2])
            for i in range(B + 3):
                if i == 3:
                    dve.wait_ge(bias_added, 2)
                if i < B:
                    dve.wait_ge(sc_mm, i + 1)
                    v.tensor_reduce(tb(0)[:, i:i + 1], PS[i % 2][0:T, 0:S], AX.X, ALU.max, negate=True
                                    ).then_inc(sc_max, 1)
                if 2 <= i <= B + 1:
                    b = i - 2
                    dve.wait_ge(sc_exp, b + 1)
                    v.reciprocal(tb(4)[:, b:b + 1], tb(1)[:, b:b + 1])
                    dve.wait_ge(pc_mm, b + 1)
                    v.tensor_copy(PC[:, :, b * T:b * T + T],
                                  PS[3][:, 0:KT * T].rearrange("p (k t) -> p k t", k=KT)
                                  ).then_inc(pc_out, 1)
                if i >= 3:
                    b = i - 3
                    dve.wait_ge(y_mm, B + b + 1)
                    dve.wait_ge(pc_out, b + 1)
                    v.scalar_tensor_tensor(out=X[:, b], in0=PS[4 + b % 2][0:T, 0:D], scalar=tb(4)[:, b:b + 1],
                                           in1=X[:, b], op0=ALU.mult, op1=ALU.add).then_inc(x_new, 1)
                    after(1, b)
            RL, DF, EX, OH, VM = tbe(5), tbe(2), tbe(3), tbe(6), tbe(7)
            dve.wait_ge(rt_mm, 1)
            dve.wait_ge(ld["rows"], 32)
            link(v.tensor_tensor(RL, PS[4][0:T, 0:B * E].rearrange("p (b e) -> p b e", b=B),
                                 BR[:].unsqueeze(1).broadcast_to([T, B, E]), ALU.add))
            link(v.tensor_reduce(tb(8), RL, AX.X, ALU.max))
            v.tensor_tensor(DF, RL, tb(8).unsqueeze(2).broadcast_to([T, B, E]), ALU.subtract
                            ).then_inc(rt_shift, 1)
            dve.wait_ge(rt_shift, 1)
            link(v.tensor_scalar(OH, DF, 0.0, None, ALU.is_ge))
            link(v.tensor_tensor(OH, OH, ev8[:], ALU.mult))
            link(v.tensor_reduce(tb(8), OH, AX.X, ALU.max))
            link(v.tensor_tensor(OH, OH, tb(8).unsqueeze(2).broadcast_to([T, B, E]), ALU.is_equal))
            oh = tiny(9).bitcast(BF16).rearrange("p (c b e) -> p c b e", c=2, b=B)
            v.memset(oh[:, 1, 0], 0.0)
            link(v.tensor_copy(oh[:, 0], OH))
            for b in range(1, B):
                ins = v.tensor_tensor(oh[:, 1, b], oh[:, 1, b - 1], oh[:, 0, b - 1], ALU.add)
                if b < B - 1:
                    link(ins)
            ins.then_inc(onehot, 1)
            GATE, POS, KEEP, SL = tb(1), tb(4), tb(10), tb(13)
            dve.wait_ge(rt_exp, 1)
            link(v.tensor_reduce(GATE, EX, AX.X, ALU.add))
            link(v.reciprocal(GATE, GATE))
            dve.wait_ge(pos_mm, 1)
            link(v.tensor_tensor(VM, OH, PS[5][0:T, 0:B * E].rearrange("p (b e) -> p b e", b=B), ALU.mult))
            link(v.tensor_reduce(POS, VM, AX.X, ALU.add))
            v.tensor_scalar(KEEP, POS, float(CAP), None, ALU.is_lt)
            v.tensor_scalar(SL, tb(8), -float(CAP), float(CAP * E), ALU.mult, ALU.add)
            link(v.tensor_scalar(tb(2), POS, float(CAP), float(4 * N), ALU.is_ge, ALU.mult))
            link(v.tensor_tensor(SL, SL, POS, ALU.add))
            v.tensor_tensor(tb(11).bitcast(I32), SL, tb(2), ALU.add)
            v.tensor_tensor(tb(12).bitcast(I32), SL, KEEP, ALU.mult).then_inc(slots_ready, 1)
            link(v.tensor_tensor(GATE, GATE, KEEP, ALU.mult))
            for b in range(B):
                v.tensor_scalar(XN[:, b], XN[:, b], GATE[:, b:b + 1], None, ALU.mult).then_inc(xg_ready, 1)
            dve.wait_ge(ld["b2"], 16)
            for e in range(E):
                dve.wait_ge(eo_mm, e + 1)
                v.tensor_tensor(EO[0:CAP, e], PS[6 + e % 2][0:CAP, 0:D], B2[0:CAP, e], ALU.add
                                ).then_inc(eo_out, 1)
            for b in range(B):
                dve.wait_ge(gat[b], 16)
                v.scalar_tensor_tensor(out=X[:, b], in0=XN[:, b], scalar=GATE[:, b:b + 1], in1=X[:, b],
                                       op0=ALU.mult, op1=ALU.add).then_inc(x_new, 1)
                after(2, b)

            def flat(t):
                return t.rearrange("p b t -> p (b t)")

            def inputs(j):
                dve.wait_ge(roots, j + 1)
                v.scalar_tensor_tensor(out=flat(UU[:, j]), in0=flat(SQ[j % 4]), scalar=1e-4, in1=flat(UU[:, j]),
                                       op0=ALU.max, op1=ALU.mult).then_inc(u_done, 1)
                dve.wait_ge(u_done, j + 1)
                v.tensor_tensor_scan(flat(UU[:, j]), flat(DEC[:, j]), flat(UU[:, j]), 0.0, ALU.mult, ALU.add
                                     ).then_inc(state, 1)

            dve.wait_ge(pads, 1)
            for j in range(RT):
                a_t = DEC[:, j, :, 1:TP]
                bt = BT[j % 2]
                dve.wait_ge(sig, 2 * j + 1)
                v.tensor_scalar(a_t, a_t, FLOOR, 1.0, ALU.max, ALU.min).then_inc(clamped, 1)
                dve.wait_ge(clamped, j + 1)
                v.tensor_scalar(bt[:, :, 1 + CHUNK:2 + CHUNK], DEC[:, j, :, 1 + CHUNK:2 + CHUNK],
                                1.0 / FLOOR, None, ALU.mult).then_inc(reset64, 1)
                dve.wait_ge(reset64, j + 1)
                v.tensor_tensor_scan(flat(CD), flat(DEC[:, j]), flat(bt), 0.0, ALU.mult, ALU.max
                                     ).then_inc(cdec, 1)
                dve.wait_ge(sig, 2 * j + 2)
                dve.wait_ge(aiv_mm, 3 * j + 3)
                for g in range(G):
                    o = UU[:, j, GB * g:GB * g + GB, 1:TP]
                    src = PS[2 * aiv_pair(3 * j + 2) + g][:, 0:GC].rearrange("p (b t) -> p b t", b=GB)
                    ins = v.tensor_tensor(o, o, src, ALU.mult)
                ins.then_inc(iv_done, 1)
                dve.wait_ge(iv_done, j + 1)
                dve.wait_ge(cdec, j + 1)
                link(v.scalar_tensor_tensor(out=flat(UU[:, j]), in0=flat(CD), scalar=1.0, in1=flat(UU[:, j]),
                                            op0=ALU.min, op1=ALU.mult))
                if j >= 4:
                    inputs(j - 4)
                if j == 1:
                    dve.wait_ge(side_out, SIDE.index(("f", 0)) + 1)
                    link(v.tensor_scalar(fs[:, 1:2], fs[:, 1:2], 1.0 / (D * D), EPS, ALU.mult, ALU.max))
                    v.tensor_scalar(fs[:, 0:1], fs[:, 1:2], 0.5, None, ALU.mult)
                    link(v.tensor_scalar(fs[:, 2:3], fs[:, 1:2], -0.5, None, ALU.mult))
                    v.tensor_scalar(WN[:], WF[:], fs[:, 0:1], fs[:, 1:2], ALU.is_gt, ALU.mult)
                    link(v.tensor_scalar(WF[:], WF[:], fs[:, 2:3], fs[:, 1:2], ALU.is_lt, ALU.mult))
                    v.tensor_tensor(WN[:], WN[:], WF[:], ALU.subtract).then_inc(wf_ready, 1)
            for j in range(RT - 4, RT):
                inputs(j)
            for b in range(B):
                add(3, b, PS[b])
            dve.wait_ge(x_new, 4 * B)
            dve.wait_ge(q4_out, 2)
            link(v.tensor_tensor(QW, QW, QP[:, 0], ALU.subtract))
            v.tensor_copy(QP[:, 1], QW).then_inc(q4_split, 1)
            dve.wait_ge(q4_split, 1)
            v.tensor_tensor(QP[:, 2], QW, QP[:, 1], ALU.subtract).then_inc(q4_split, 1)
            v.memset(PS[6], 0.0).then_inc(pv_zero, 1)

            def row_max(b, i):
                w = PAIRS * b + i
                dve.wait_ge(mx_mm, w + 1)
                if i == 0 and b >= 2:
                    dve.wait_ge(np_ready, b - 1)
                v.tensor_reduce(NM[:, b % 2, 2 * i:2 * i + 2], PP[w % 2][0:T, :, 0:S], AX.X, ALU.max, negate=True
                                ).then_inc(mx_out, 1)

            def normalise(b, _):
                dve.wait_ge(os_tr, b + 1)
                if b >= 1:
                    dve.wait_ge(on_tr, b)
                o = PS[7][0:T, 0:H * VW].rearrange("p (h w) -> p h w", h=H)
                link(v.reciprocal(RC4[:], o[:, :, DK]))
                v.tensor_tensor(ON, o[:, :, 0:DK], RC4[:].unsqueeze(2).broadcast_to([T, H, DK]), ALU.mult
                                ).then_inc(on_ready, 1)

            run_block4(maxima=row_max, normalise=normalise, add=lambda b, _: add(4, b, Y4))
            for b in range(B):
                add(5, b, PS[4 + b % 4])


_OUT = (B, T, D)


def kernel(**inputs):
    import concourse.bacc as bacc
    from concourse.bass_utils import run_bass_kernel_spmd

    nc = bacc.Bacc("TRN2", target_bir_lowering=False, num_devices=1)
    x = {n: np.asarray(v) for n, v in inputs.items()}

    def cols(v):
        return v.reshape(-1, P).T

    laid = {n: x[n] for n in ("x", "ctx_1024", "mask_BxS2_ik1", "L0_attn_Wq", "L0_attn_Wk", "L0_attn_Wv",
                              "L0_attn_Wo", "L0_xattn_Wv", "L0_ffn_Wr", "L0_ffn_br", "L0_ffn_W1", "L0_ffn_W2",
                              "L0_ffn_b2", "L1_attn_W_aiv", "L1_attn_W_mix")}
    laid["mask_keep"] = x["mask_BxS2_bk0"].reshape(-1).view(np.uint32)
    laid["ctx_t"] = x["ctx_1024"].transpose(2, 0, 1).reshape(D, B * S)
    laid["wqx_t"] = x["L0_xattn_Wq"].T
    laid["wkx_t"] = x["L0_xattn_Wk"].T
    laid["wk1_t"] = x["L1_xattn_Wk"].T
    laid["wv1_t"] = x["L1_xattn_Wv"].T
    laid["wq1_t"] = x["L1_xattn_Wq"].T
    laid["wo1_t"] = x["L1_xattn_Wo"].T
    laid["wf_t"] = x["L1_ffn_weight"].T
    laid["pos9"] = np.concatenate([x["L0_attn_pos_emb"][0][:, :NPOS]] * HH, axis=0)
    laid["colbias"] = np.concatenate([cols(x[n]) for n in (
        "L0_attn_bq", "L0_attn_bk", "L0_attn_bv", "L0_xattn_bq", "L1_xattn_bk", "L1_xattn_bq", "L1_xattn_bv",
        "L1_attn_decay_bias", "L0_ffn_b1")], axis=1)
    laid["rowbias"] = np.stack([x[n] for n in ("L0_attn_bo", "L0_xattn_bv", "L1_attn_b_mix", "L1_xattn_bo")])
    arrays, aps = {}, {}
    for n, v in laid.items():
        v = np.ascontiguousarray(v)
        arrays["in_" + n] = v
        aps[n] = nc.dram_tensor("in_" + n, v.shape, mybir.dt.from_np(v.dtype), kind="ExternalInput").ap()
    out = nc.dram_tensor("out_x", _OUT, F32, kind="ExternalOutput").ap()
    build(nc, aps, out)
    r = run_bass_kernel_spmd(nc, [arrays], core_ids=[0])
    return r.results[0]["out_x"]
```
